# Optimizing a Trainium2 kernel written in Bass

```python
import numpy as np
import jax
import jax.numpy as jnp

def _softmax(x, axis=-1):
    return jax.nn.softmax(x, axis=axis)

def _gelu(x):
    return jax.nn.gelu(x, approximate=True)

def _silu(x):
    return jax.nn.silu(x)

def _sigmoid(x):
    return jax.nn.sigmoid(x)

def _layernorm(x, axis=-1, eps=1e-05):
    m = jnp.mean(x, axis=axis, keepdims=True)
    v = jnp.var(x, axis=axis, keepdims=True)
    return (x - m) / jnp.sqrt(v + eps)

def _scatter_add(tgt, idx, src, axis=0):
    return tgt.at[idx].add(src)

def _segment_sum(src, seg, n):
    return jax.ops.segment_sum(src, seg, n)
kernel_name = 'mk_vit_tower_cls_d1_tok_img1024_r4_4b55e5'

def setup_inputs(seed: int=0):
    np.random.seed(seed)
    _w = jnp.asarray

    def _rec_inputs():
        import jax
        import jax.numpy as jnp
        _rk = jax.random.key(seed)
        x = -7.10856e-05 + 0.999911 * jax.random.normal(jax.random.fold_in(_rk, 1), (4, 1, 1024, 256), jnp.float32)
        cls_tok = 0.02 * jax.random.normal(jax.random.fold_in(_rk, 5), (1, 1, 256), jnp.float32)
        return (x, cls_tok)
    x, cls_tok = _rec_inputs()

    def _L0_tok_setup():
        import jax, jax.numpy as jnp
        import numpy as np
        B, T, X, D, H = (16, 1, 1024, 256, 128)
        key = jax.random.key(seed)
        k0, k1, k2 = jax.random.split(key, 3)
        s1 = 1.0 / np.sqrt(D)
        s2 = 1.0 / np.sqrt(H)
        return {'encoder_outputs': jax.random.normal(k0, (B, T, X, D), dtype=jnp.float32), 'W1': jax.random.uniform(k1, (D, H), minval=-s1, maxval=s1, dtype=jnp.float32), 'b1': jnp.zeros((H,), dtype=jnp.float32), 'W2': jax.random.uniform(k2, (H, 1), minval=-s2, maxval=s2, dtype=jnp.float32), 'b2': jnp.zeros((1,), dtype=jnp.float32)}
    _L0_tok_all = _L0_tok_setup()
    _L0_tok_in = {k: v for k, v in _L0_tok_all.items() if k in ('W1', 'b1', 'W2', 'b2')}
    del _L0_tok_all

    def _L0_attn_setup():
        import jax, jax.numpy as jnp
        import numpy as np
        B, N, D = (2, 512, 256)
        H, DH = (16, 64)
        SOFTCLAMP = 50.0
        SCALE = DH ** (-0.5)
        key = jax.random.key(seed)
        ks = jax.random.split(key, 5)
        std = D ** (-0.5)
        return {'x': jax.random.normal(ks[0], (B, N, D), dtype=jnp.float32), 'Wq': jax.random.normal(ks[1], (H * DH, D), dtype=jnp.float32) * std, 'Wk': jax.random.normal(ks[2], (H * DH, D), dtype=jnp.float32) * std, 'Wv': jax.random.normal(ks[3], (H * DH, D), dtype=jnp.float32) * std, 'Wo': jax.random.normal(ks[4], (D, H * DH), dtype=jnp.float32) * std}
    _L0_attn_all = _L0_attn_setup()
    _L0_attn_in = {k: v for k, v in _L0_attn_all.items() if k in ('Wq', 'Wk', 'Wv', 'Wo')}
    del _L0_attn_all

    def _L0_ffn_setup():
        import jax, jax.numpy as jnp
        import numpy as np
        D_MODEL = 256
        D_FF = 1024
        N_EXPERTS = 8
        TOP_K = 2
        LN_EPS = 1e-06

        def _moe(x, router_w, w1, b1, w2, b2, gamma, beta):
            B, S, D = x.shape
            x_flat = x.reshape(-1, D)
            N = x_flat.shape[0]
            logits = x_flat @ router_w
            gate_vals, gate_idx = jax.lax.top_k(logits, TOP_K)
            gate_w = jax.nn.softmax(gate_vals, axis=-1)
            gates = jnp.zeros_like(logits).at[jnp.arange(N)[:, None], gate_idx].set(gate_w)
            h = jax.nn.gelu(jnp.einsum('nd,edf->enf', x_flat, w1) + b1[:, None, :], approximate=False)
            out = jnp.einsum('enf,efd->end', h, w2) + b2[:, None, :]
            res = x_flat[None, :, :] + out
            mu = jnp.mean(res, axis=-1, keepdims=True)
            var = jnp.mean(jnp.square(res - mu), axis=-1, keepdims=True)
            normed = (res - mu) * jax.lax.rsqrt(var + LN_EPS)
            expert_out = normed * gamma[:, None, :] + beta[:, None, :]
            y = jnp.einsum('end,ne->nd', expert_out, gates)
            return y.reshape(B, S, D)
        key = jax.random.key(seed)
        ks = jax.random.split(key, 8)
        x = jax.random.normal(ks[0], (2, 512, D_MODEL), dtype=jnp.float32)
        router_w = jax.random.normal(ks[1], (D_MODEL, N_EXPERTS), dtype=jnp.float32) * 0.02
        w1 = jax.random.normal(ks[2], (N_EXPERTS, D_MODEL, D_FF), dtype=jnp.float32) * 0.02
        b1 = jnp.zeros((N_EXPERTS, D_FF), dtype=jnp.float32)
        w2 = jax.random.normal(ks[3], (N_EXPERTS, D_FF, D_MODEL), dtype=jnp.float32) * 0.02
        b2 = jnp.zeros((N_EXPERTS, D_MODEL), dtype=jnp.float32)
        gamma = jnp.ones((N_EXPERTS, D_MODEL), dtype=jnp.float32)
        beta = jnp.zeros((N_EXPERTS, D_MODEL), dtype=jnp.float32)
        return {'x': x, 'router_w': router_w, 'w1': w1, 'b1': b1, 'w2': w2, 'b2': b2, 'gamma': gamma, 'beta': beta}
    _L0_ffn_all = _L0_ffn_setup()
    _L0_ffn_in = {k: v for k, v in _L0_ffn_all.items() if k in ('router_w', 'w1', 'b1', 'w2', 'b2', 'gamma', 'beta')}
    del _L0_ffn_all
    return {'x': x, 'cls_tok': cls_tok, 'L0_tok_W1': _L0_tok_in['W1'], 'L0_tok_b1': _L0_tok_in['b1'], 'L0_tok_W2': _L0_tok_in['W2'], 'L0_tok_b2': _L0_tok_in['b2'], 'L0_attn_Wq': _L0_attn_in['Wq'], 'L0_attn_Wk': _L0_attn_in['Wk'], 'L0_attn_Wv': _L0_attn_in['Wv'], 'L0_attn_Wo': _L0_attn_in['Wo'], 'L0_ffn_router_w': _L0_ffn_in['router_w'], 'L0_ffn_w1': _L0_ffn_in['w1'], 'L0_ffn_b1': _L0_ffn_in['b1'], 'L0_ffn_w2': _L0_ffn_in['w2'], 'L0_ffn_b2': _L0_ffn_in['b2'], 'L0_ffn_gamma': _L0_ffn_in['gamma'], 'L0_ffn_beta': _L0_ffn_in['beta']}

def reference(x, cls_tok, L0_tok_W1, L0_tok_b1, L0_tok_W2, L0_tok_b2, L0_attn_Wq, L0_attn_Wk, L0_attn_Wv, L0_attn_Wo, L0_ffn_router_w, L0_ffn_w1, L0_ffn_b1, L0_ffn_w2, L0_ffn_b2, L0_ffn_gamma, L0_ffn_beta):
    import jax
    import jax.numpy as jnp

    def _L0_tok_ref(encoder_outputs, W1, b1, W2, b2):
        import jax, jax.numpy as jnp
        import numpy as np
        B, T, X, D, H = (16, 1, 1024, 256, 128)
        h = jnp.tanh(encoder_outputs @ W1 + b1)
        energy = h @ W2 + b2
        energy = jnp.transpose(energy, (0, 3, 2, 1))
        weights = jax.nn.softmax(jnp.squeeze(energy, -1), axis=1)
        out = (encoder_outputs * weights[..., None]).sum(axis=1)
        return out

    def _L0_attn_ref(x, Wq, Wk, Wv, Wo):
        import jax, jax.numpy as jnp
        import numpy as np
        B, N, D = (2, 512, 256)
        H, DH = (16, 64)
        SOFTCLAMP = 50.0
        SCALE = DH ** (-0.5)
        b, n, _ = x.shape
        q = jnp.einsum('bnd,fd->bnf', x, Wq).reshape(b, n, H, DH).transpose(0, 2, 1, 3)
        k = jnp.einsum('bnd,fd->bnf', x, Wk).reshape(b, n, H, DH).transpose(0, 2, 1, 3)
        v = jnp.einsum('bnd,fd->bnf', x, Wv).reshape(b, n, H, DH).transpose(0, 2, 1, 3)
        sim = jnp.einsum('bhid,bhjd->bhij', q, k) * SCALE
        sim = SOFTCLAMP * jnp.tanh(sim / SOFTCLAMP)
        causal = jnp.tril(jnp.ones((n, n), dtype=bool))
        sim = jnp.where(causal, sim, jnp.finfo(sim.dtype).min)
        attn = jax.nn.softmax(sim, axis=-1)
        out = jnp.einsum('bhij,bhjd->bhid', attn, v)
        out = out.transpose(0, 2, 1, 3).reshape(b, n, H * DH)
        return jnp.einsum('bnf,df->bnd', out, Wo)

    def _L0_ffn_ref(x, router_w, w1, b1, w2, b2, gamma, beta):
        import jax, jax.numpy as jnp
        import numpy as np
        D_MODEL = 256
        D_FF = 1024
        N_EXPERTS = 8
        TOP_K = 2
        LN_EPS = 1e-06

        def _moe(x, router_w, w1, b1, w2, b2, gamma, beta):
            B, S, D = x.shape
            x_flat = x.reshape(-1, D)
            N = x_flat.shape[0]
            logits = x_flat @ router_w
            gate_vals, gate_idx = jax.lax.top_k(logits, TOP_K)
            gate_w = jax.nn.softmax(gate_vals, axis=-1)
            gates = jnp.zeros_like(logits).at[jnp.arange(N)[:, None], gate_idx].set(gate_w)
            h = jax.nn.gelu(jnp.einsum('nd,edf->enf', x_flat, w1) + b1[:, None, :], approximate=False)
            out = jnp.einsum('enf,efd->end', h, w2) + b2[:, None, :]
            res = x_flat[None, :, :] + out
            mu = jnp.mean(res, axis=-1, keepdims=True)
            var = jnp.mean(jnp.square(res - mu), axis=-1, keepdims=True)
            normed = (res - mu) * jax.lax.rsqrt(var + LN_EPS)
            expert_out = normed * gamma[:, None, :] + beta[:, None, :]
            y = jnp.einsum('end,ne->nd', expert_out, gates)
            return y.reshape(B, S, D)
        return _moe(x, router_w, w1, b1, w2, b2, gamma, beta)
    h = _L0_tok_ref(x, L0_tok_W1, L0_tok_b1, L0_tok_W2, L0_tok_b2)
    h = jnp.concatenate([jnp.broadcast_to(cls_tok, (h.shape[0], 1, h.shape[2])), h], axis=1)
    h = h + _L0_attn_ref(_layernorm(h, axis=-1), L0_attn_Wq, L0_attn_Wk, L0_attn_Wv, L0_attn_Wo)
    h = h + _L0_ffn_ref(_layernorm(h, axis=-1), L0_ffn_router_w, L0_ffn_w1, L0_ffn_b1, L0_ffn_w2, L0_ffn_b2, L0_ffn_gamma, L0_ffn_beta)
    return h

_drawn_inputs = setup_inputs


def setup_inputs(seed=0):
    import zlib

    import numpy as np

    out = dict(_drawn_inputs(seed))
    spreads = {'L0_tok_b1': (0.0, 0.1),
     'L0_ffn_b1': (0.0, 0.606),
     'L0_ffn_b2': (0.0, 0.1),
     'L0_ffn_gamma': (1.0, 0.2),
     'L0_ffn_beta': (0.0, 0.1)}
    factors = {}
    for name, (base, spread) in spreads.items():
        noise = np.random.default_rng([zlib.crc32(name.encode()), seed]).standard_normal(out[name].shape)
        drawn = base * np.exp(spread * noise) if base else spread * noise
        out[name] = jnp.asarray(drawn.astype(out[name].dtype))
    for name, factor in factors.items():
        out[name] = (out[name] * factor).astype(out[name].dtype)
    return out
```

```python
from contextlib import ExitStack

import concourse.bass as bass
from concourse import mybir

F32 = mybir.dt.float32
F32R = mybir.dt.float32r
I32 = mybir.dt.int32
U32 = mybir.dt.uint32
ALU = mybir.AluOpType
ACT = mybir.ActivationFunctionType
AX = mybir.AxisListType

P = 128
B = 4
X = 1024
T = X + 1
D = 256
C = D // P
DH = 64
PAIRS = 8
KT = 9
TP = KT * P
TQ = T + 3
QC = 344
QW = [QC, QC, TQ - 2 * QC]
TAIL = TQ - (T - 1)
NE = 8
F = 1024
FM = F // P
CLAMP = 50.0
SCALE = DH ** -0.5
LN1_EPS = 1e-5
LN2_EPS = 1e-6

TT = 384
TS = TT // P
MAXT = -(-B * T // TT)
NTILE = (2 * B * T + NE * (TT - 1)) // TT
REGION = MAXT * TT + TT
SPARE = NE * REGION
TRASH = SPARE + TT
ROWS = TRASH + 2 * P
ROW, TOK, G2, DG, E1 = D + 4, D, D + 1, D + 2, D + 3



def make_slots():
    s = [dict(n=QC, halves=[(0, 0, 0), (0, 0, QC)]),
         dict(n=QC, halves=[(1, 0, 0), (1, 0, QC)]),
         dict(n=QW[2], halves=[(0, 0, 2 * QC), (1, 0, 2 * QC)])]
    for i in range(1, KT - 1):
        w = TQ - P * i
        if w > 512:
            for h in range(2):
                s.append(dict(n=w // 2, halves=[(h, i, P * i), (h, i, P * i + w // 2)]))
        elif i < KT - 2:
            s.append(dict(n=w, halves=[(0, i, P * i), (1, i, P * i)]))
        else:
            s.append(dict(n=w + TAIL, halves=[(0, i, P * i), (1, i, P * i)], tail=TAIL))
    return s


SLOTS = make_slots()
NS = len(SLOTS)
PMAX = max(2 * s["n"] for s in SLOTS)
PRING = 7
assert (2 * NS) % PRING == 0 and NS % 2 == 0
UNITS = [[n for n, s in enumerate(SLOTS) if s["halves"][0][1] == i] for i in range(KT - 1)]
NU = len(UNITS)
UNIT_OF = {n: u for u, ns in enumerate(UNITS) for n in ns}
DIAG = [n for n in range(NS) if n != 2]
CHUNK_UNIT = [2, 5, 7]
CHUNK_SLOT = [max(UNITS[u]) for u in CHUNK_UNIT]


def masks_through(n):
    return sum(1 for m in DIAG if m <= n)


def sums_through(n):
    return n + 1 + (n == NS - 1)


SUMS = sums_through(NS - 1)
ECHAIN = 31
CHAIN = 145


def pv_pieces(u):
    by_head = [[], []]
    for n in UNITS[u]:
        s = SLOTS[n]
        tail = s.get("tail", 0)
        for k, (h, i, q0) in enumerate(s["halves"]):
            runs = [(i, q0, q0 + s["n"] - tail, k * s["n"])]
            if tail:
                runs.append((i + 1, T - 1, TQ, (k + 1) * s["n"] - tail))
            for i_, a, b, col in runs:
                while a < b:
                    c = a // QC
                    e = min(b, (c + 1) * QC)
                    by_head[h].append((n, col, h, i_, c, a, e))
                    col += e - a
                    a = e
    return [p for pair in zip(*by_head) for p in pair]


AUX_PROJ = 9
JOBS = [("q", 0), ("q", 1), ("q", 2), ("k", 0), ("k", 1), ("k", 2), ("v", 0), ("den", 0),
        ("v", 1), ("v", 2), ("den", 1), ("den", 2)]
NJ = len(JOBS)
AUX_BATCH = AUX_PROJ + (PAIRS - 1) * NJ + 3


def job_step(j):
    kind, c = JOBS[j]
    if kind == "den":
        return [11, NS, NS + 2][c]
    return {"q": [0, 1, 2], "k": [3, 4, 5], "v": [6, 12, NS - 1]}[kind][c]


def attention(nc, io, xs, out, keep):
    x, cls, wqkv, wot, router = io["x"], io["cls"], io["wqkv"], io["wot"], io["router"]
    with ExitStack() as ctx:
        def sb(name, shape, dt=F32):
            return ctx.enter_context(nc.sbuf_tensor(name, shape, dt))

        def sem(name):
            return ctx.enter_context(nc.semaphore(name))

        H = sb("H", [P, KT, D])
        XN = sb("XN", [P, KT, ROW])
        xnT = sb("xnT", [P, C, TP])
        W = [sb(f"W{j}", [P, 3, C, P]) for j in range(2)]
        WO = sb("WO", [P, PAIRS, D])
        R = sb("R", [P, C, NE])
        qN = sb("qN", [P, 2, TQ], F32R)
        kN = sb("kN", [P, 2, TQ], F32R)
        q4 = [sb(f"q4_{j}", [P, 2, 2, TQ], F32R) for j in range(2)]
        kS = [sb(f"kS_{j}", [P, 2, TP], F32R) for j in range(2)]
        V = [sb(f"V_{j}", [P, KT, P]) for j in range(2)]
        TH = sb("TH", [P, 2, PMAX])
        PR = sb("PR", [P, PRING, PMAX])
        SUM = sb("SUM", [P, 2, TQ])
        RC = sb("RC", [P, QC])
        OT = sb("OT", [P, PAIRS, TQ])
        ident = sb("ident", [P, P])
        ones = sb("ones", [P, P])
        upper = sb("upper", [P, P])
        st = sb("st", [P, KT, 6])
        mv = sb("mv", [P, KT, 2])
        rs = sb("rs", [P, KT])
        vh = sb("vh", [P, KT])
        nt = sb("nt", [P, KT])
        lg = sb("lg", [P, KT, NE])
        top = sb("top", [P, KT, NE])
        ti = sb("ti", [P, KT, NE], U32)
        tf = sb("tf", [P, KT, 2])
        M = sb("M", [P, 2, KT, NE])
        CC = sb("CC", [P, KT, NE])
        rank = sb("rank", [P, KT, NE])
        mr = sb("mr", [P, 2, KT, NE])
        pf = sb("pf", [P, 2, KT])
        pi = sb("pi", [P, 2, KT], I32)
        eg = sb("eg", [P, 2, KT])
        gate = sb("gate", [P, KT])
        iota_e = sb("iota_e", [P, KT, NE])
        valid = sb("valid", [P, KT, NE])
        trash = sb("trash", [P, 2, KT])
        tok = sb("tok", [P, KT])
        run = keep["run"]

        S = ctx.enter_context(nc.psum_tensor("S", [P, 4, 512], F32))
        O = ctx.enter_context(nc.psum_tensor("O", [P, 3, 512], F32))
        AUX = ctx.enter_context(nc.psum_tensor("AUX", [P, 512], F32))

        s_const = sem("s_const")
        s_zero = sem("s_zero")
        s_wo = sem("s_wo")
        s_w = [sem("s_w0"), sem("s_w1")]
        s_h = sem("s_h")
        s_dve = sem("s_dve")
        s_xn = sem("s_xn")
        s_xt = sem("s_xt")
        s_xnT = sem("s_xnT")
        s_aux = sem("s_aux")
        s_hi = sem("s_hi")
        s_evac = sem("s_evac")
        s_qd = sem("s_qd")
        s_kd = sem("s_kd")
        s_qk = sem("s_qk")
        s_th = sem("s_th")
        s_ex = sem("s_ex")
        s_mask = sem("s_mask")
        s_sum = sem("s_sum")
        s_pv = sem("s_pv")
        s_norm = sem("s_norm")
        s_y = sem("s_y")
        s_h2 = sem("s_h2")
        s_lg = sem("s_lg")
        s_ge = sem("s_ge")
        s_cc = sem("s_cc")
        s_rank = sem("s_rank")
        s_pos = sem("s_pos")
        s_sc = sem("s_sc")
        s_hs = sem("s_hs")
        s_apart = sem("s_apart")

        def apart(eng):
            eng.sem_inc(s_apart, 1)

        block = ctx.enter_context(nc.Block())

        @block.sync
        def _(sp):
            sp.dma_start(WO[:], wot).then_inc(s_wo, 16)
            sp.dma_start(R[:], router).then_inc(s_wo, 16)
            for j in range(2):
                sp.dma_start(W[j][:], wqkv[j]).then_inc(s_w[j], 16)
            sp.wait_ge(s_zero, 1)

            def spread(j, g, done):
                def half(dst, src, s):
                    sp.dma_start(dst.bitcast(F32), src.bitcast(F32)).then_inc(s, 16)

                sp.wait_ge(s_evac, done + 3)
                for h in range(2):
                    for o in range(2):
                        half(q4[j][64 * o:64 * o + 64, h], qN[64 * h:64 * h + 64], s_qd)
                sp.wait_ge(s_evac, done + 6)
                for h in range(2):
                    for part in range(2):
                        half(kS[j][64 * part:64 * part + 64, h, 0:TQ],
                             kN[64 * h:64 * h + 64, part], s_kd)

            with sp.Fori(0, B) as b:
                sp.wait_ge(s_hs, b * 32)
                apart(sp)
                sp.wait_ge(s_xn, 2 * b)
                sp.dma_start(H[0:1, 0], cls).then_inc(s_h, 16)
                sp.dma_start(H[1:P, 0], x[b, 0:P - 1]).then_inc(s_h, 16)
                sp.dma_start(H[:, 1:KT - 1],
                             x[b, P - 1:X - 1].rearrange("(t p) d -> p t d", p=P)).then_inc(s_h, 16)
                sp.dma_start(H[0:1, KT - 1], x[b, X - 1:X]).then_inc(s_h, 16)
                spread(0, b * PAIRS, b * AUX_BATCH)

                def pair(pp, j, last=False):
                    base = b * AUX_BATCH + AUX_PROJ + (2 * pp + j) * NJ
                    sp.wait_ge(s_aux, base)
                    sp.dma_start(W[j][:], wqkv[2 * pp + j + 2]).then_inc(s_w[j], 16)
                    if not last:
                        spread(1 - j, None, base)

                with sp.Fori(0, PAIRS // 2 - 1) as pp:
                    pair(pp, 0)
                    pair(pp, 1)
                pair(PAIRS // 2 - 1, 0)
                pair(PAIRS // 2 - 1, 1, last=True)
                sp.wait_ge(s_h2, (b + 1) * KT)
                sp.dma_start(out[bass.ds(b * T, X)].rearrange("(t p) d -> p t d", p=P),
                             H[:, 0:KT - 1]).then_inc(s_hs, 16)
                sp.dma_start(out[bass.ds(b * T + X, 1)], H[0:1, KT - 1]).then_inc(s_hs, 16)
            sp.wait_ge(s_hs, B * 32)
            for j in range(2):
                sp.wait_ge(s_w[j], 16 * (B * PAIRS // 2 + 1))

        @block.gpsimd
        def _(pool):
            nc.gpsimd.memset(ones[:], 1.0).then_inc(s_const, 1)
            pool.wait_ge(s_const, 1)
            nc.gpsimd.affine_select(out=ident[:], in_=ones[:], compare_op=ALU.is_equal, fill=0.0,
                                    base=0, pattern=[[-1, P]], channel_multiplier=1).then_inc(s_const, 1)
            nc.gpsimd.affine_select(out=upper[:], in_=ones[:], compare_op=ALU.is_gt, fill=0.0,
                                    base=0, pattern=[[1, P]], channel_multiplier=-1).then_inc(s_const, 1)
            nc.gpsimd.iota(iota_e[:], pattern=[[0, KT], [1, NE]], base=0, channel_multiplier=0,
                           allow_small_or_imprecise_dtypes=True).then_inc(s_const, 1)
            nc.gpsimd.memset(valid[:], 1.0).then_inc(s_const, 1)
            pool.wait_ge(s_const, 5)
            nc.gpsimd.affine_select(out=valid[:, KT - 1], in_=valid[:, KT - 1], compare_op=ALU.is_ge,
                                    fill=0.0, base=0, pattern=[[0, NE]],
                                    channel_multiplier=-1).then_inc(s_const, 1)
            nc.gpsimd.iota(trash[:], pattern=[[P, 2], [0, KT]], base=TRASH, channel_multiplier=1,
                           allow_small_or_imprecise_dtypes=True).then_inc(s_const, 1)
            pool.wait_ge(s_const, 7)
            nc.gpsimd.memset(trash[:, :, 0:KT - 1], 0.0).then_inc(s_const, 1)
            nc.gpsimd.memset(trash[0:1, :, KT - 1:KT], 0.0).then_inc(s_const, 1)
            nc.gpsimd.iota(tok[:], pattern=[[P, KT]], base=0, channel_multiplier=1,
                           allow_small_or_imprecise_dtypes=True).then_inc(s_const, 1)

            def pair(b, g):
                for n in DIAG:
                    s = SLOTS[n]
                    h0, h1 = s["halves"]
                    pool.wait_ge(s_ex, g * NS + n + 1)
                    apart(pool)
                    pr = PR[:, (base_slot + n) % PRING, 0:2 * s["n"]]
                    if h0[0] == h1[0]:
                        v, pat = pr[:, 0:P], [[1, P]]
                    else:
                        v = pr.rearrange("p (h q) -> p h q", h=2)[:, :, 0:P]
                        pat = [[0, 2], [1, P]]
                    nc.gpsimd.affine_select(out=v, in_=v, compare_op=ALU.is_ge, fill=0.0, base=0,
                                            pattern=pat, channel_multiplier=-1).then_inc(s_mask, 1)

            with pool.Fori(0, B) as b:
                with pool.Fori(0, PAIRS // 2) as pp:
                    for j in range(2):
                        base_slot = j * NS
                        pair(b, b * PAIRS + 2 * pp + j)
                pool.wait_ge(s_pos, b + 1)
                apart(pool)
                for t in range(KT):
                    for k in range(2):
                        nc.gpsimd.indirect_dma_start(
                            xs, bass.IndirectOffsetOnAxis(pi[:, k, t:t + 1], 0),
                            XN[:, t], None).then_inc(s_sc, 16)
            pool.wait_ge(s_sc, B * KT * 2 * 16)

        @block.scalar
        def _(act):
            act.sem_inc(s_th, 2)

            def hi(k, c, g, done, first_wait):
                dst, s = ((qN, s_qd), (kN, s_kd))[k]
                act.wait_ge(s_aux, done)
                if c == 0:
                    act.wait_ge(s, g * 64)
                nc.scalar.copy(dst[:, 0, c * QC:c * QC + QW[c]], AUX[:, 0:QW[c]]).then_inc(s_hi, 1)

            def tanh(g, n, base):
                s = SLOTS[n]
                act.wait_ge(s_qk, g * NS + n + 1)
                act.wait_ge(s_ex, g * NS + n - 1 if n >= 2 else g * NS)
                nc.scalar.activation(
                    TH[:, n % 2, 0:2 * s["n"]].rearrange("p (h q) -> p h q", h=2),
                    S[:, 2 * (n % 2):2 * (n % 2) + 2, 0:s["n"]], ACT.Tanh,
                    scale=SCALE / CLAMP).then_inc(s_th, 1)

            def exp(g, n, base):
                s = SLOTS[n]
                act.wait_ge(s_th, 2 + g * NS + n + 1)
                m = n - PRING
                if m >= 0:
                    act.wait_ge(s_pv, NU + g * NU + UNIT_OF[m] + 1)
                    act.wait_ge(s_sum, SUMS + g * SUMS + sums_through(m))
                else:
                    act.wait_ge(s_pv, g * NU + UNIT_OF[m + NS] + 1)
                    act.wait_ge(s_sum, g * SUMS + sums_through(m + NS))
                nc.scalar.activation(PR[:, (base + n) % PRING, 0:2 * s["n"]],
                                     TH[:, n % 2, 0:2 * s["n"]], ACT.Exp,
                                     scale=CLAMP).then_inc(s_ex, 1)

            def pair(b, pp, j, last=False):
                p = 2 * pp + j
                g = b * PAIRS + p
                done = b * AUX_BATCH + AUX_PROJ + p * NJ
                for n in range(NS + 1):
                    if n < NS:
                        tanh(g, n, j * NS)
                    if n >= 1:
                        exp(g, n - 1, j * NS)
                    for jj, (kind, c) in enumerate(JOBS):
                        if kind in "qk" and job_step(jj) == n and not last:
                            hi("qk".index(kind), c, g + 1, done + jj + 1, None)

            with act.Fori(0, B) as b:
                for jj in range(6):
                    hi(jj // 3, jj % 3, b * PAIRS, b * AUX_BATCH + jj + 1, None)
                with act.Fori(0, PAIRS // 2 - 1) as pp:
                    pair(b, pp, 0)
                    pair(b, pp, 1)
                pair(b, PAIRS // 2 - 1, 0)
                pair(b, PAIRS // 2 - 1, 1, last=True)
                act.wait_ge(s_ge, 2 * b + 1)
                nc.scalar.activation(eg[:, 0], eg[:, 1], ACT.Exp).then_inc(s_ge, 1)

        @block.tensor
        def _(pe):
            def qk(g, j, n):
                s = SLOTS[n]
                if n == 0:
                    pe.wait_ge(s_qd, 64 * (g + 1))
                    pe.wait_ge(s_kd, 64 * (g + 1))
                pe.wait_ge(s_th, g * NS + n + 1)
                tail = s.get("tail", 0)
                for k, (h, i, q0) in enumerate(s["halves"]):
                    out = S[:, 2 * (n % 2) + k]
                    runs = [(i, q0, 0, s["n"] - tail)]
                    if tail:
                        runs.append((i + 1, T - 1, s["n"] - tail, s["n"]))
                    for i_, q, a, e in runs:
                        for part in range(2):
                            mm = nc.tensor.matmul(out[:, a:e], kS[j][:, h, P * i_:P * i_ + P],
                                                  q4[j][:, h, part, q:q + e - a],
                                                  start=(part == 0), stop=(part == 1))
                mm.then_inc(s_qk, 1)

            def pv(g, j, u, done):
                n = max(UNITS[u])
                if u == 0:
                    pe.wait_ge(s_evac, done)
                    pe.wait_ge(s_norm, 3 * g)
                    pe.wait_ge(s_ex, g * NS + n + 1)
                pe.wait_ge(s_mask, g * len(DIAG) + masks_through(n))
                for n_, col, h, i, c, a, e in pv_pieces(u):
                    K = 1 if i == KT - 1 else P
                    last = i == CHUNK_LAST[c]
                    mm = nc.tensor.matmul(O[64 * h:64 * h + 64, c, a - c * QC:e - c * QC],
                                          V[j][0:K, i, 64 * h:64 * h + 64],
                                          PR[0:K, (j * NS + n_) % PRING, col:col + e - a],
                                          start=(i == 0), stop=last, skip_group_check=True)
                mm.then_inc(s_pv, 1)

            CHUNK_LAST = [2, 5, KT - 1]

            def job(kind, c, j, g, done):
                pe.wait_ge(s_evac, done)
                if kind in "qk":
                    w = "qk".index(kind)
                    if kind == "q" and c == 0:
                        pe.wait_ge(s_w[j], 16 * g)
                    for ci in range(C):
                        mm = nc.tensor.matmul(AUX[:, 0:QW[c]], W[j][:, w, ci],
                                              xnT[:, ci, c * QC:c * QC + QW[c]],
                                              start=(ci == 0), stop=(ci == C - 1))
                elif kind == "v":
                    for t in range(3):
                        for ci in range(C):
                            tok = P * (3 * c + t)
                            mm = nc.tensor.matmul(AUX[:, P * t:P * t + P], xnT[:, ci, tok:tok + P],
                                                  W[j][:, 2, ci], start=(ci == 0), stop=(ci == C - 1))
                else:
                    pe.wait_ge(s_sum, SUMS + (g * SUMS) + sums_through(CHUNK_SLOT[c]))
                    for h in range(2):
                        mm = nc.tensor.matmul(AUX[64 * h:64 * h + 64, 0:QW[c]], ones[:, 0:64],
                                              SUM[:, h, c * QC:c * QC + QW[c]],
                                              start=True, stop=True, skip_group_check=True)
                mm.then_inc(s_aux, 1)

            def pair(b, pp, j, last=False):
                p = 2 * pp + j
                g = b * PAIRS + p
                done = b * AUX_BATCH + AUX_PROJ + p * NJ
                nxt = b * (PAIRS // 2) + pp + 1 + j

                def jobs_at(step):
                    for jj, (kind, c) in enumerate(JOBS):
                        if job_step(jj) == step:
                            if kind == "den":
                                job(kind, c, j, g, done + (c if last else jj))
                            elif not last:
                                job(kind, c, 1 - j, nxt, done + jj)

                def units_at(step):
                    for u in range(NU):
                        if max(UNITS[u]) + 2 == step and u < NU - 3:
                            pv(g, j, u, done)

                for n in range(NS):
                    qk(g, j, n)
                    units_at(n)
                    jobs_at(n)
                pv(g, j, NU - 3, done)
                jobs_at(NS)
                pv(g, j, NU - 2, done)
                jobs_at(NS + 1)
                pv(g, j, NU - 1, done)
                jobs_at(NS + 2)

            def transposes(n):
                pe.wait_ge(s_xn, n)
                for ci in range(C):
                    for t in range(KT):
                        out = (S[:, 2 * ci + t // 4, P * (t % 4):P * (t % 4) + P] if t < KT - 1
                               else O[:, 0, P * ci:P * ci + P])
                        mm = nc.tensor.transpose(out, XN[:, t, P * ci:P * ci + P], ident[:])
                mm.then_inc(s_xt, 1)

            pe.sem_inc(s_pv, NU)
            pe.wait_ge(s_const, 10)
            pe.wait_ge(s_wo, 32)
            with pe.Fori(0, B) as b:
                transposes(2 * b + 1)
                pe.wait_ge(s_xnT, 2 * b + 1)
                for jj in range(AUX_PROJ):
                    job("qkv"[jj // 3], jj % 3, 0, 4 * b + 1, b * AUX_BATCH + jj)
                with pe.Fori(0, PAIRS // 2 - 1) as pp:
                    pair(b, pp, 0)
                    pair(b, pp, 1)
                pair(b, PAIRS // 2 - 1, 0)
                pair(b, PAIRS // 2 - 1, 1, last=True)
                pe.wait_ge(s_th, 2 + (b + 1) * PAIRS * NS)
                pe.wait_ge(s_norm, 3 * PAIRS * (b + 1))
                for t in range(KT):
                    if t >= 4:
                        pe.wait_ge(s_h2, b * KT + t - 3)
                    m = P if t < KT - 1 else 1
                    for p in range(PAIRS):
                        mm = nc.tensor.matmul(S[0:m, t % 4, 0:D], OT[:, p, P * t:P * t + m], WO[:, p],
                                              start=(p == 0), stop=(p == PAIRS - 1))
                    mm.then_inc(s_y, 1)
                pe.wait_ge(s_h2, (b + 1) * KT)
                transposes(2 * b + 2)
                pe.wait_ge(s_xnT, 2 * b + 2)
                for t in range(KT):
                    for ci in range(C):
                        mm = nc.tensor.matmul(O[:, 1, NE * t:NE * t + NE], xnT[:, ci, P * t:P * t + P],
                                              R[:, ci], start=(ci == 0), stop=(ci == C - 1))
                mm.then_inc(s_lg, 1)
                pe.wait_ge(s_cc, b + 1)
                nc.tensor.matmul(O[:, 2, 0:KT * NE], upper[:], CC[:].rearrange("p t e -> p (t e)"),
                                 start=True, stop=True)
                nc.tensor.matmul(O[:, 2, 128:128 + KT * NE], ones[:], CC[:].rearrange("p t e -> p (t e)"),
                                 start=True, stop=True).then_inc(s_rank, 1)
                pe.wait_ge(s_pos, b + 1)

        @block.vector
        def _(dve):
            v = nc.vector
            zeros = [H[:, KT - 1], run[:], ]
            for j in range(2):
                zeros.append(kS[j][:, :, T:TP].bitcast(F32))
            for z in zeros:
                v.memset(z, 0.0).then_inc(s_dve, 1)
            dve.wait_ge(s_dve, len(zeros))
            dve.sem_inc(s_zero, 1)
            dve.sem_inc(s_sum, SUMS)
            dve.wait_ge(s_const, 10)
            count = [0]

            def link(ins):
                count[0] += 1
                ins.then_inc(s_dve, 1)
                dve.wait_ge(s_dve, chain_base + count[0])

            def layernorm(b, n):
                for t in range(KT):
                    ins = v.bn_stats(st[:, t], H[:, t])
                    if t < KT - 1:
                        ins.then_inc(s_dve, 1)
                        count[0] += 1
                link(ins)
                apart(dve)
                for t in range(KT):
                    ins = v.bn_aggr(mv[:, t], st[:, t])
                    if t < KT - 1:
                        ins.then_inc(s_dve, 1)
                        count[0] += 1
                link(ins)
                rsqrt_steps(v, link, mv[:, :, 1], rs, vh, nt, LN1_EPS)
                for t in range(KT):
                    ins = v.tensor_scalar(XN[:, t, 0:D], H[:, t], mv[:, t, 0:1], rs[:, t:t + 1],
                                          ALU.subtract, ALU.mult)
                    ins.then_inc(s_dve, 1)
                    count[0] += 1
                dve.wait_ge(s_dve, chain_base + count[0])
                dve.sem_inc(s_xn, 1)

            def turned(b, n):
                dve.wait_ge(s_xt, n)
                v.tensor_copy(xnT[:, :, 0:X].rearrange("p c (k q) -> p c k q", k=2),
                              S[:].rearrange("p (c k) q -> p c k q", c=C)).then_inc(s_dve, 1)
                v.tensor_copy(xnT[:, :, X:TP], O[:, 0, 0:2 * P].rearrange("p (c q) -> p c q", c=C)).then_inc(s_dve, 1)
                count[0] += 2
                dve.wait_ge(s_dve, chain_base + count[0])
                dve.sem_inc(s_xnT, 1)

            def read_out(kind, c, j, done, g):
                dve.wait_ge(s_aux, done + 1)
                cols = slice(c * QC, c * QC + QW[c])
                if kind in "qk":
                    dst = (qN, kN)["qk".index(kind)]
                    dve.wait_ge(s_hi, 6 * g + 3 * "qk".index(kind) + c + 1)
                    v.tensor_tensor(dst[:, 1, cols], AUX[:, 0:QW[c]], dst[:, 0, cols].bitcast(F32),
                                    ALU.subtract).then_inc(s_evac, 1)
                elif kind == "v":
                    v.tensor_copy(V[j][:, 3 * c:3 * c + 3],
                                  AUX[:, 0:3 * P].rearrange("p (t f) -> p t f", t=3)).then_inc(s_evac, 1)

            def sums(g, j, n, done):
                s = SLOTS[n]
                (h0, i, q0), (h1, _, q1) = s["halves"]
                w, tail = s["n"], s.get("tail", 0)
                if n in DIAG:
                    dve.wait_ge(s_mask, g * len(DIAG) + masks_through(n))
                else:
                    dve.wait_ge(s_ex, g * NS + n + 1)
                pr = PR[:, (j * NS + n) % PRING, 0:2 * w]
                if h0 == h1:
                    dst = SUM[:, h0, q0:q0 + 2 * w]
                else:
                    pr = pr.rearrange("p (h q) -> p h q", h=2)
                    dst = SUM[:, :, q0:q0 + w - tail]
                if i == 0:
                    dve.wait_ge(s_aux, done)
                    v.tensor_copy(dst, pr).then_inc(s_sum, 1)
                    return
                dve.wait_ge(s_sum, SUMS + g * SUMS + (n if h0 != h1 else max(n - 1, 3)))
                src = pr if h0 == h1 else pr[:, :, 0:w - tail]
                v.tensor_tensor(dst, dst, src, ALU.add).then_inc(s_sum, 1)
                if tail:
                    dve.wait_ge(s_sum, SUMS + g * SUMS + n + 1)
                    dst = SUM[0:1, :, T - 1:TQ]
                    v.tensor_tensor(dst, dst, pr[0:1, :, w - tail:w], ALU.add).then_inc(s_sum, 1)

            def normalise(b, g, p, c, done):
                dve.wait_ge(s_aux, done + 1)
                dve.wait_ge(s_norm, 3 * g + c)
                v.reciprocal(RC[:, 0:QW[c]], AUX[:, 0:QW[c]]).then_inc(s_evac, 1)
                dve.wait_ge(s_evac, done + 1)
                dve.wait_ge(s_pv, NU + g * NU + CHUNK_UNIT[c] + 1)
                v.tensor_tensor(OT[:, bass.ds(p, 1), c * QC:c * QC + QW[c]].rearrange("p a q -> p (a q)"),
                                O[:, c, 0:QW[c]], RC[:, 0:QW[c]], ALU.mult).then_inc(s_norm, 1)

            def pair(b, pp, j, last=False):
                p = 2 * pp + j
                g = b * PAIRS + p
                done = b * AUX_BATCH + AUX_PROJ + p * NJ

                def jobs_at(step):
                    for jj, (kind, c) in enumerate(JOBS):
                        if job_step(jj) != step:
                            continue
                        if kind == "den":
                            normalise(b, g, p, c, done + (c if last else jj))
                        elif not last:
                            read_out(kind, c, 1 - j, done + jj, g + 1)

                for n in range(NS + 3):
                    if n < NS:
                        if n >= 1:
                            sums(g, j, n - 1, done)
                        jobs_at(n)
                    elif n == NS:
                        sums(g, j, NS - 1, done)
                        jobs_at(n)
                    else:
                        jobs_at(n)

            with dve.Fori(0, B) as b:
                chain_base = len(zeros) + b * CHAIN
                count[0] = 0
                dve.wait_ge(s_h, 64 * (b + 1))
                dve.wait_ge(s_sc, b * KT * 2 * 16)
                layernorm(b, 2 * b + 1)
                turned(b, 2 * b + 1)
                for jj in range(AUX_PROJ):
                    read_out("qkv"[jj // 3], jj % 3, 0, b * AUX_BATCH + jj, b * PAIRS)
                dve.wait_ge(s_y, b * KT)
                apart(dve)
                with dve.Fori(0, PAIRS // 2 - 1) as pp:
                    pair(b, pp, 0)
                    pair(b, pp, 1)
                pair(b, PAIRS // 2 - 1, 0)
                pair(b, PAIRS // 2 - 1, 1, last=True)
                for t in range(KT):
                    m = P if t < KT - 1 else 1
                    dve.wait_ge(s_y, b * KT + t + 1)
                    v.tensor_tensor(H[0:m, t], H[0:m, t], S[0:m, t % 4, 0:D], ALU.add).then_inc(s_h2, 1)
                dve.wait_ge(s_h2, (b + 1) * KT)
                layernorm(b, 2 * b + 2)
                turned(b, 2 * b + 2)
                dve.wait_ge(s_lg, b + 1)
                link(v.tensor_copy(lg[:].rearrange("p t e -> p (t e)"), O[:, 1, 0:KT * NE]))
                apart(dve)
                for t in range(KT):
                    ins = v.max(top[:, t], lg[:, t])
                    ins.then_inc(s_dve, 1)
                    count[0] += 1
                dve.wait_ge(s_dve, chain_base + count[0])
                apart(dve)
                for t in range(KT):
                    ins = v.max_index(ti[:, t], top[:, t], lg[:, t])
                    ins.then_inc(s_dve, 1)
                    count[0] += 1
                dve.wait_ge(s_dve, chain_base + count[0])
                v.tensor_tensor(eg[:, 1], top[:, :, 1], top[:, :, 0], ALU.subtract).then_inc(s_ge, 1)
                link(v.tensor_copy(tf[:], ti[:, :, 0:2]))
                for k in range(2):
                    link(v.tensor_tensor(M[:, k], iota_e[:], tf[:, :, k:k + 1].to_broadcast([P, KT, NE]),
                                         ALU.is_equal))
                for k in range(2):
                    link(v.tensor_tensor(M[:, k], M[:, k], valid[:], ALU.mult))
                v.tensor_tensor(CC[:], M[:, 0], M[:, 1], ALU.add).then_inc(s_cc, 1)
                dve.wait_ge(s_ge, 2 * b + 2)
                link(v.tensor_scalar(eg[:, 1], eg[:, 0], 1.0, None, ALU.add))
                link(v.reciprocal(gate[:], eg[:, 1]))
                link(v.tensor_tensor(XN[:, :, G2], gate[:], eg[:, 0], ALU.mult))
                link(v.tensor_tensor(XN[:, :, DG], gate[:], XN[:, :, G2], ALU.subtract))
                link(v.tensor_copy(XN[:, :, E1], tf[:, :, 0]))
                link(v.tensor_copy(XN[:, :, TOK], tok[:]))
                link(v.tensor_scalar(tok[:], tok[:], float(T), None, ALU.add))
                dve.wait_ge(s_rank, b + 1)
                for t in range(KT):
                    link(v.tensor_tensor(rank[:, t], O[:, 2, NE * t:NE * t + NE], run[:], ALU.add))
                    link(v.tensor_tensor(run[:], run[:], O[:, 2, 128 + NE * t:128 + NE * t + NE], ALU.add))
                link(v.scalar_tensor_tensor(out=rank[:], in0=iota_e[:], scalar=float(REGION),
                                            in1=rank[:], op0=ALU.mult, op1=ALU.add))
                for k in range(2):
                    link(v.tensor_tensor(mr[:, k], M[:, k], rank[:], ALU.mult))
                link(v.tensor_reduce(pf[:], mr[:], AX.X, ALU.add))
                link(v.tensor_tensor(pf[:], pf[:], trash[:], ALU.add))
                link(v.tensor_copy(pi[:], pf[:]))
                dve.sem_inc(s_pos, 1)
                assert count[0] == CHAIN, count[0]




def rsqrt_steps(v, link, var, y, h, t, eps):
    link(v.tensor_scalar(h[:], var, eps, None, ALU.add))
    link(v.tensor_scalar(t[:].bitcast(I32), h[:].bitcast(I32), 1, None, ALU.arith_shift_right))
    link(v.tensor_scalar(y[:].bitcast(I32), t[:].bitcast(I32), -1.0, float(0x5F3759DF), ALU.mult, ALU.add))
    link(v.tensor_scalar(h[:], h[:], -0.5, None, ALU.mult))
    for _ in range(4):
        link(v.tensor_tensor(t[:], y[:], y[:], ALU.mult))
        link(v.tensor_tensor(t[:], t[:], h[:], ALU.mult))
        link(v.scalar_tensor_tensor(out=y[:], in0=t[:], scalar=1.5, in1=y[:], op0=ALU.add, op1=ALU.mult))


def experts(nc, io, xs, out, keep):
    w1, b1, w2, bc = io["w1"], io["b1"], io["w2"], io["bc"]
    run = keep["run"]
    with ExitStack() as ctx:
        def sb(name, shape, dt=F32):
            return ctx.enter_context(nc.sbuf_tensor(name, shape, dt))

        def sem(name):
            return ctx.enter_context(nc.semaphore(name))

        def pair_of(name, shape, dt=F32):
            return [sb(f"{name}{j}", shape, dt) for j in range(2)]

        def sems(name):
            return [sem(f"{name}{j}") for j in range(2)]

        ident = sb("ident2", [P, P])
        ones = sb("ones2", [P, P])
        fill = sb("fill", [P, TS, ROW])
        thr = sb("thr", [P, NE, MAXT])
        cmp = sb("cmp", [P, NE, MAXT])
        nt = sb("ntiles", [P, NE])
        ce = sb("ce", [P, NE])
        ci = sb("ci", [P, NE])
        tid = sb("tid", [P, NTILE, NE])
        eid = sb("eid", [P, NTILE, NE])
        a = sb("a", [P, NTILE, NE])
        z = sb("z", [P, NTILE, NE])
        EF = sb("EF", [P, NTILE])
        SF = sb("SF", [P, NTILE])
        EI = sb("EI", [P, NTILE], I32)
        SI = sb("SI", [P, NTILE], I32)
        zf = sb("zf", [P, NE])
        ZI = sb("ZI", [P, NE], I32)
        eb = sb("eb", [P, NE])

        XR = pair_of("XR", [P, TS, ROW])
        W1 = pair_of("W1_", [P, C, F])
        W2 = pair_of("W2_", [P, FM, D])
        B1 = pair_of("B1_", [P, FM])
        BC = pair_of("BC_", [P, 3, D])
        xT = pair_of("xT_", [P, C, TT])
        hT = sb("hT", [P, FM, TT])
        XB = sb("XB", [P, TS, D])
        RES = sb("RES", [P, TS, D])
        NRM = sb("NRM", [P, TS, D])
        GM = sb("GM", [P, TS, D])
        OUT = pair_of("OUT_", [P, TS, D])
        IDX = pair_of("IDX_", [P, TS], I32)
        st = sb("st2", [P, TS, 6])
        mv = sb("mv2", [P, TS, 2])
        rs = sb("rs2", [P, TS])
        vh = sb("vh2", [P, TS])
        tt_ = sb("tt2", [P, TS])
        g = sb("g2", [P, TS])
        rg = sb("rg2", [P, TS])

        H1 = ctx.enter_context(nc.psum_tensor("H1", [P, 4, 512], F32))
        Y2 = ctx.enter_context(nc.psum_tensor("Y2", [P, TS, 512], F32))
        XP = ctx.enter_context(nc.psum_tensor("XP", [P, 512], F32))

        s_const = sem("e_const")
        s_list = sem("e_list")
        s_fill = sem("e_fill")
        s_x = sems("e_x")
        s_w = sems("e_w")
        s_xp = sem("e_xp")
        s_xT = sem("e_xT")
        s_m1 = sem("e_m1")
        s_ge = sem("e_ge")
        s_m2 = sem("e_m2")
        s_xb = sem("e_xb")
        s_res = sem("e_res")
        s_ch = sem("e_ch")
        s_nrm = sem("e_nrm")
        s_gm = sem("e_gm")
        s_out = sem("e_out")
        s_apart = sem("e_apart")
        s_add = sem("e_add")
        s_clear = sem("e_clear")

        def apart(eng):
            eng.sem_inc(s_apart, 1)

        block = ctx.enter_context(nc.Block())
        HALF = NTILE // 2
        assert NTILE % 2 == 1
        LIST = 31

        @block.sync
        def _(sp):
            sp.wait_ge(s_const, 7)
            sp.dma_start(xs[SPARE:SPARE + TT].rearrange("(t p) d -> p t d", p=P), fill[:]).then_inc(s_fill, 16)
            sp.dma_start(out[B * T:B * T + TT].rearrange("(t p) d -> p t d", p=P),
                         fill[:, :, 0:D]).then_inc(s_fill, 16)
            sp.wait_ge(s_list, LIST)
            with sp.Fori(0, NE) as e:
                row = sp.value_load(ZI[0:1, bass.ds(e, 1)], min_val=0, max_val=SPARE - TT)
                sp.dma_start(xs[bass.ds(row, TT)].rearrange("(t p) d -> p t d", p=P), fill[:]).then_inc(s_fill, 16)
            sp.wait_ge(s_fill, 16 * (2 + NE))

            def load(t, j, k):
                if k is not None:
                    sp.wait_ge(s_out, t - 1)
                row = sp.value_load(SI[0:1, bass.ds(t, 1)], min_val=0, max_val=SPARE)
                e = sp.value_load(EI[0:1, bass.ds(t, 1)], min_val=0, max_val=NE - 1)
                sp.dma_start(XR[j][:], xs[bass.ds(row, TT)].rearrange("(t p) d -> p t d", p=P)).then_inc(s_x[j], 16)
                sp.dma_start(W1[j][:], w1[bass.ds(e, 1)].rearrange("a (c p) f -> p (a c) f", p=P)).then_inc(s_w[j], 16)
                sp.dma_start(B1[j][:], b1[bass.ds(e, 1)].rearrange("a p m -> p (a m)")).then_inc(s_w[j], 16)
                sp.dma_start(W2[j][:], w2[bass.ds(e, 1)].rearrange("a (m p) d -> p (a m) d", p=P)).then_inc(s_w[j], 16)
                sp.dma_start(BC[j][:], bc[bass.ds(e, 1)].to_broadcast([P, 3, D])).then_inc(s_w[j], 16)

            load(0, 0, None)
            load(1, 1, None)
            with sp.Fori(1, HALF) as k:
                load(2 * k, 0, k)
                load(2 * k + 1, 1, k)
            load(NTILE - 1, 0, HALF)

        @block.gpsimd
        def _(pool):
            nc.gpsimd.memset(ones[:], 1.0).then_inc(s_const, 1)
            nc.gpsimd.memset(fill[:], 0.0).then_inc(s_const, 1)
            pool.wait_ge(s_const, 2)
            nc.gpsimd.affine_select(out=ident[:], in_=ones[:], compare_op=ALU.is_equal, fill=0.0,
                                    base=0, pattern=[[-1, P]], channel_multiplier=1).then_inc(s_const, 1)
            nc.gpsimd.iota(fill[:, :, TOK], pattern=[[P, TS]], base=B * T, channel_multiplier=1,
                           allow_small_or_imprecise_dtypes=True).then_inc(s_const, 1)
            nc.gpsimd.iota(thr[:], pattern=[[0, NE], [TT, MAXT]], base=0, channel_multiplier=0,
                           allow_small_or_imprecise_dtypes=True).then_inc(s_const, 1)
            nc.gpsimd.iota(tid[:], pattern=[[1, NTILE], [0, NE]], base=0, channel_multiplier=0,
                           allow_small_or_imprecise_dtypes=True).then_inc(s_const, 1)
            nc.gpsimd.iota(eid[:], pattern=[[0, NTILE], [REGION, NE]], base=0, channel_multiplier=0,
                           allow_small_or_imprecise_dtypes=True).then_inc(s_const, 1)

            def bias(t, j, k):
                pool.wait_ge(s_x[j], 16 * (k + 1))
                pool.wait_ge(s_w[j], 64 * (k + 1))
                pool.wait_ge(s_res, t)
                nc.gpsimd.tensor_tensor(XB[:], XR[j][:, :, 0:D], BC[j][:, 0:1].to_broadcast([P, TS, D]),
                                        ALU.add).then_inc(s_xb, 1)

            def scale(t, j):
                pool.wait_ge(s_nrm, t + 1)
                pool.wait_ge(s_out, t)
                nc.gpsimd.tensor_tensor(GM[:], NRM[:], BC[j][:, 1:2].to_broadcast([P, TS, D]),
                                        ALU.mult).then_inc(s_gm, 1)

            def add(t, j):
                pool.wait_ge(s_out, t + 1)
                pool.wait_ge(s_add, 16 * TS * t)
                pool.sem_inc(s_clear, 1)
                for k in range(TS):
                    nc.gpsimd.indirect_dma_start(out, bass.IndirectOffsetOnAxis(IDX[j][:, k:k + 1], 0),
                                                 OUT[j][:, k], None, compute_op=ALU.add).then_inc(s_add, 16)

            def tile(t, j, k):
                bias(t, j, k)
                scale(t, j)
                add(t, j)

            with pool.Fori(0, HALF) as k:
                tile(2 * k, 0, k)
                tile(2 * k + 1, 1, k)
            tile(NTILE - 1, 0, HALF)
            pool.wait_ge(s_add, 16 * TS * NTILE)

        @block.scalar
        def _(act):
            act.sem_inc(s_ge, 4)

            def tile(t, j, k):
                act.wait_ge(s_w[j], 64 * (k + 1))
                for m in range(FM):
                    act.wait_ge(s_m1, FM * t + m + 1)
                    nc.scalar.activation(hT[:, m], H1[:, m % 4, 0:TT], ACT.Gelu,
                                         bias=B1[j][:, m:m + 1]).then_inc(s_ge, 1)

            with act.Fori(0, HALF) as k:
                tile(2 * k, 0, k)
                tile(2 * k + 1, 1, k)
            tile(NTILE - 1, 0, HALF)

        @block.tensor
        def _(pe):
            pe.wait_ge(s_const, 7)

            def turn(t, j, k, c):
                if c == 0:
                    pe.wait_ge(s_x[j], 16 * (k + 1))
                pe.wait_ge(s_xT, C * t + c)
                for i in range(TS):
                    mm = nc.tensor.transpose(XP[:, P * i:P * i + P], XR[j][:, i, P * c:P * c + P], ident[:])
                mm.then_inc(s_xp, 1)

            def tile(t, j, k, kn):
                pe.wait_ge(s_w[j], 64 * (k + 1))
                pe.wait_ge(s_xT, C * t + C)
                for m in range(FM):
                    pe.wait_ge(s_ge, FM * t + m + 1)
                    for c in range(C):
                        mm = nc.tensor.matmul(H1[:, m % 4, 0:TT], W1[j][:, c, P * m:P * m + P], xT[j][:, c],
                                              start=(c == 0), stop=(c == C - 1))
                    mm.then_inc(s_m1, 1)
                    if kn is not None and m in (3, FM - 1):
                        turn(t + 1, 1 - j, kn, m // 4)
                pe.wait_ge(s_res, t)
                for m in range(FM):
                    pe.wait_ge(s_ge, 4 + FM * t + m + 1)
                    for i in range(TS):
                        mm = nc.tensor.matmul(Y2[:, i, 0:D], hT[:, m, P * i:P * i + P], W2[j][:, m],
                                              start=(m == 0), stop=(m == FM - 1))
                mm.then_inc(s_m2, 1)

            turn(0, 0, 0, 0)
            turn(0, 0, 0, 1)
            with pe.Fori(0, HALF) as k:
                tile(2 * k, 0, k, k)
                tile(2 * k + 1, 1, k, k + 1)
            tile(NTILE - 1, 0, HALF, None)

        @block.vector
        def _(dve):
            v = nc.vector
            count = [0]
            base = [0]
            chain = [s_list]

            def link(ins):
                count[0] += 1
                ins.then_inc(chain[0], 1)
                dve.wait_ge(chain[0], base[0] + count[0])

            def wide(ap):
                return ap[:].rearrange("p (o e) -> p o e", o=1).to_broadcast([P, NTILE, NE])

            dve.wait_ge(s_const, 7)
            link(v.tensor_tensor(cmp[:], run[:].rearrange("p (e o) -> p e o", o=1).to_broadcast([P, NE, MAXT]),
                                 thr[:], ALU.is_gt))
            link(v.tensor_reduce(nt[:], cmp[:], AX.X, ALU.add))
            link(v.tensor_copy(ci[:], nt[:]))
            for e in range(1, NE):
                link(v.tensor_tensor(ci[:, e:e + 1], ci[:, e:e + 1], ci[:, e - 1:e], ALU.add))
            link(v.tensor_tensor(ce[:], ci[:], nt[:], ALU.subtract))
            link(v.tensor_tensor(a[:], tid[:], wide(ci), ALU.is_ge))
            link(v.tensor_reduce(EF[:], a[:], AX.X, ALU.add))
            link(v.tensor_scalar(EF[:], EF[:], float(NE - 1), None, ALU.min))
            link(v.tensor_tensor(z[:], tid[:], wide(ce), ALU.is_ge))
            link(v.tensor_tensor(a[:], z[:], a[:], ALU.subtract))
            link(v.tensor_tensor(z[:], tid[:], wide(ce), ALU.subtract))
            link(v.scalar_tensor_tensor(out=z[:], in0=z[:], scalar=float(TT), in1=eid[:],
                                        op0=ALU.mult, op1=ALU.add))
            link(v.tensor_scalar(z[:], z[:], float(SPARE), None, ALU.subtract))
            link(v.tensor_tensor(z[:], z[:], a[:], ALU.mult))
            link(v.tensor_reduce(SF[:], z[:], AX.X, ALU.add))
            link(v.tensor_scalar(SF[:], SF[:], float(SPARE), None, ALU.add))
            link(v.tensor_copy(SI[:], SF[:]))
            link(v.tensor_copy(EI[:], EF[:]))
            link(v.tensor_tensor(zf[:], run[:], eid[:, 0], ALU.add))
            link(v.tensor_copy(ZI[:], zf[:]))
            assert count[0] <= LIST, count[0]
            dve.sem_inc(s_list, LIST - count[0])
            chain[0] = s_ch

            def turned(t, j, c):
                dve.wait_ge(s_xp, C * t + c + 1)
                v.tensor_copy(xT[j][:, c], XP[:, 0:TT]).then_inc(s_xT, 1)

            def tile(t, j, k, last=False):
                base[0] = t * ECHAIN
                count[0] = 0
                if not last:
                    turned(t + 1, 1 - j, 0)
                    turned(t + 1, 1 - j, 1)
                dve.wait_ge(s_out, t)
                link(v.tensor_scalar(g[:], XR[j][:, :, E1], EF[:, bass.ds(t, 1)], None, ALU.is_equal))
                link(v.tensor_tensor(g[:], g[:], XR[j][:, :, DG], ALU.mult))
                link(v.tensor_tensor(g[:], g[:], XR[j][:, :, G2], ALU.add))
                dve.wait_ge(s_clear, t)
                link(v.tensor_copy(IDX[j][:], XR[j][:, :, TOK]))
                dve.wait_ge(s_xb, t + 1)
                dve.wait_ge(s_m2, t + 1)
                v.tensor_tensor(RES[:], Y2[:, :, 0:D], XB[:], ALU.add).then_inc(s_res, 1)
                dve.wait_ge(s_res, t + 1)
                for i in range(TS):
                    ins = v.bn_stats(st[:, i], RES[:, i])
                    if i < TS - 1:
                        ins.then_inc(s_ch, 1)
                        count[0] += 1
                link(ins)
                apart(dve)
                for i in range(TS):
                    ins = v.bn_aggr(mv[:, i], st[:, i])
                    if i < TS - 1:
                        ins.then_inc(s_ch, 1)
                        count[0] += 1
                link(ins)
                rsqrt_steps(v, link, mv[:, :, 1], rs, vh, tt_, LN2_EPS)
                link(v.tensor_tensor(rg[:], rs[:], g[:], ALU.mult))
                dve.wait_ge(s_gm, t)
                for i in range(TS):
                    ins = v.tensor_scalar(NRM[:, i], RES[:, i], mv[:, i, 0:1], rg[:, i:i + 1],
                                          ALU.subtract, ALU.mult)
                    if i < TS - 1:
                        ins.then_inc(s_ch, 1)
                        count[0] += 1
                ins.then_inc(s_nrm, 1)
                dve.wait_ge(s_gm, t + 1)
                for i in range(TS):
                    ins = v.scalar_tensor_tensor(out=OUT[j][:, i], in0=BC[j][:, 2], scalar=g[:, i:i + 1],
                                                 in1=GM[:, i], op0=ALU.mult, op1=ALU.add)
                    if i < TS - 1:
                        ins.then_inc(s_ch, 1)
                        count[0] += 1
                ins.then_inc(s_out, 1)
                assert count[0] == ECHAIN, count[0]

            turned(0, 0, 0)
            turned(0, 0, 1)
            with dve.Fori(0, HALF) as k:
                tile(2 * k, 0, k)
                tile(2 * k + 1, 1, k)
            tile(NTILE - 1, 0, HALF, last=True)


def build(nc, io, xs, out):
    with ExitStack() as ctx:
        keep = {"run": ctx.enter_context(nc.sbuf_tensor("run", [P, NE], F32))}
        attention(nc, io, xs, out, keep)
        experts(nc, io, xs, out, keep)


def kernel(x, cls_tok, L0_tok_W1, L0_tok_b1, L0_tok_W2, L0_tok_b2, L0_attn_Wq, L0_attn_Wk, L0_attn_Wv,
           L0_attn_Wo, L0_ffn_router_w, L0_ffn_w1, L0_ffn_b1, L0_ffn_w2, L0_ffn_b2, L0_ffn_gamma,
           L0_ffn_beta):
    import numpy as np
    import concourse.bacc as bacc
    from concourse.bass_utils import run_bass_kernel_spmd

    def by_pair(w):
        return np.asarray(w).reshape(PAIRS, P, C, P).transpose(0, 3, 2, 1)

    wqkv = np.stack([by_pair(w) for w in (L0_attn_Wq, L0_attn_Wk, L0_attn_Wv)], axis=2)
    arrays = {
        "x": np.asarray(x).reshape(B, X, D),
        "cls": np.asarray(cls_tok).reshape(1, D),
        "wqkv": np.concatenate([wqkv, wqkv[:2]]),
        "wot": np.asarray(L0_attn_Wo).T.reshape(PAIRS, P, D).transpose(1, 0, 2),
        "router": np.asarray(L0_ffn_router_w).reshape(C, P, NE).transpose(1, 0, 2),
        "w1": np.asarray(L0_ffn_w1),
        "b1": np.asarray(L0_ffn_b1).reshape(NE, FM, P).transpose(0, 2, 1),
        "w2": np.asarray(L0_ffn_w2),
        "bc": np.stack([np.asarray(a) for a in (L0_ffn_b2, L0_ffn_gamma, L0_ffn_beta)], axis=1),
    }
    arrays = {k: np.ascontiguousarray(a) for k, a in arrays.items()}
    nc = bacc.Bacc("TRN2", target_bir_lowering=False, num_devices=1)
    io = {k: nc.dram_tensor(f"in_{k}", list(a.shape), F32, kind="ExternalInput").ap() for k, a in arrays.items()}
    xs = nc.dram_tensor("rows", [ROWS, ROW], F32, kind="Internal").ap()
    out = nc.dram_tensor("out", [B * T + TT, D], F32, kind="ExternalOutput").ap()
    build(nc, io, xs, out)
    r = run_bass_kernel_spmd(nc, [{f"in_{k}": a for k, a in arrays.items()}], core_ids=[0])
    return r.results[0]["out"][0:B * T].reshape(B, T, D)
```

```python
from contextlib import ExitStack

import concourse.bass as bass
from concourse import mybir

F32 = mybir.dt.float32
F32R = mybir.dt.float32r
I32 = mybir.dt.int32
U32 = mybir.dt.uint32
ALU = mybir.AluOpType
ACT = mybir.ActivationFunctionType
AX = mybir.AxisListType

P = 128
B = 4
X = 1024
T = X + 1
D = 256
C = D // P
DH = 64
PAIRS = 8
KT = 9
TP = KT * P
TQ = T + 3
QC = 344
QW = [QC, QC, TQ - 2 * QC]
TAIL = TQ - (T - 1)
NE = 8
F = 1024
FM = F // P
CLAMP = 50.0
SCALE = DH ** -0.5
LN1_EPS = 1e-5
LN2_EPS = 1e-6

TT = 384
TS = TT // P
MAXT = -(-B * T // TT)
NTILE = (2 * B * T + NE * (TT - 1)) // TT
REGION = MAXT * TT + TT
SPARE = NE * REGION
TRASH = SPARE + TT
ROWS = TRASH + 2 * P
ROW, TOK, G2, DG, E1 = D + 4, D, D + 1, D + 2, D + 3



def make_slots():
    s = [dict(n=QC, halves=[(0, 0, 0), (0, 0, QC)]),
         dict(n=QC, halves=[(1, 0, 0), (1, 0, QC)]),
         dict(n=QW[2], halves=[(0, 0, 2 * QC), (1, 0, 2 * QC)])]
    for i in range(1, KT - 1):
        w = TQ - P * i
        if w > 512:
            for h in range(2):
                s.append(dict(n=w // 2, halves=[(h, i, P * i), (h, i, P * i + w // 2)]))
        elif i < KT - 2:
            s.append(dict(n=w, halves=[(0, i, P * i), (1, i, P * i)]))
        else:
            s.append(dict(n=w + TAIL, halves=[(0, i, P * i), (1, i, P * i)], tail=TAIL))
    return s


SLOTS = make_slots()
NS = len(SLOTS)
PMAX = max(2 * s["n"] for s in SLOTS)
THRING = 2
PRING = 7
assert (2 * NS) % PRING == 0 and NS % 2 == 0
UNITS = [[n for n, s in enumerate(SLOTS) if s["halves"][0][1] == i] for i in range(KT - 1)]
NU = len(UNITS)
UNIT_OF = {n: u for u, ns in enumerate(UNITS) for n in ns}
DIAG = [n for n in range(NS) if n != 2]
CHUNK_UNIT = [2, 5, 7]
CHUNK_SLOT = [max(UNITS[u]) for u in CHUNK_UNIT]


def masks_through(n):
    return sum(1 for m in DIAG if m <= n)


DSUMS = 9


def pool_sums_through(n):
    return n + 1 - DSUMS + (n == NS - 1)


PSUMS = pool_sums_through(NS - 1)
HRING = 4
ECHAIN = 28
CHAIN = 139


def pv_pieces(u):
    by_head = [[], []]
    for n in UNITS[u]:
        s = SLOTS[n]
        tail = s.get("tail", 0)
        for k, (h, i, q0) in enumerate(s["halves"]):
            runs = [(i, q0, q0 + s["n"] - tail, k * s["n"])]
            if tail:
                runs.append((i + 1, T - 1, TQ, (k + 1) * s["n"] - tail))
            for i_, a, b, col in runs:
                while a < b:
                    c = a // QC
                    e = min(b, (c + 1) * QC)
                    by_head[h].append((n, col, h, i_, c, a, e))
                    col += e - a
                    a = e
    return [p for pair in zip(*by_head) for p in pair]


UNIT_AT = {0: (5, -1), 1: (6, -1), 2: (7, -1), 6: (0, 0), 7: (1, 0), 9: (2, 0), 11: (3, 0), 13: (4, 0)}
JOB_AT = {0: ("q", 0), 1: ("den", 1), 3: ("den", 2), 4: ("q", 1), 5: ("q", 2), 6: ("k", 0), 7: ("k", 1),
          8: ("k", 2), 9: ("v", 0), 10: ("v", 1), 11: ("den", 0), 12: ("v", 2)}
PROJ = [(k, c) for k in "qkv" for c in range(3)]
AUX_FIRST = len(PROJ) + len(JOB_AT) - 2
AUX_LAST = AUX_FIRST + (PAIRS - 2) * len(JOB_AT)
AUX_BATCH = AUX_LAST + 5


def has_job(step, kind):
    if step not in JOB_AT:
        return False
    what, c = JOB_AT[step]
    return not (kind == "first" and what == "den" and c > 0) and not (kind == "last" and what != "den")


def jobs_before(step, kind):
    return sum(has_job(n, kind) for n in range(step))


def attention(nc, io, xs, out, keep):
    x, cls, wqkv, wot, router = io["x"], io["cls"], io["wqkv"], io["wot"], io["router"]
    with ExitStack() as ctx:
        def sb(name, shape, dt=F32):
            return ctx.enter_context(nc.sbuf_tensor(name, shape, dt))

        def sem(name):
            return ctx.enter_context(nc.semaphore(name))

        H = sb("H", [P, KT, D])
        XN = sb("XN", [P, KT, ROW])
        xnT = sb("xnT", [P, C, TP])
        W = [sb(f"W{j}", [P, 3, C, P]) for j in range(2)]
        WO = sb("WO", [P, PAIRS, D])
        R = sb("R", [P, C, NE])
        raw = sb("raw", [P, 2, QC])
        qN = sb("qN", [P, 2, TQ], F32R)
        kN = sb("kN", [P, 2, TQ], F32R)
        q4 = [sb(f"q4_{j}", [P, 2, 2, TQ], F32R) for j in range(2)]
        kS = [sb(f"kS_{j}", [P, 2, TP], F32R) for j in range(2)]
        V = [sb(f"V_{j}", [P, KT, P]) for j in range(2)]
        TH = sb("TH", [P, THRING, PMAX])
        PR = sb("PR", [P, PRING, PMAX])
        SUM = sb("SUM", [P, 2, TQ])
        RC = sb("RC", [P, QC])
        OT = sb("OT", [P, PAIRS, TQ])
        ident = sb("ident", [P, P])
        ones = sb("ones", [P, P])
        upper = sb("upper", [P, P])
        st = sb("st", [P, KT, 6])
        mv = sb("mv", [P, KT, 2])
        rs = sb("rs", [P, KT])
        vh = sb("vh", [P, KT])
        nt = sb("nt", [P, KT])
        lg = sb("lg", [P, KT, NE])
        top = sb("top", [P, KT, NE])
        ti = sb("ti", [P, KT, NE], U32)
        tf = sb("tf", [P, KT, 2])
        M = sb("M", [P, 2, KT, NE])
        CC = sb("CC", [P, KT, NE])
        rank = sb("rank", [P, KT, NE])
        mr = sb("mr", [P, 2, KT, NE])
        pf = sb("pf", [P, 2, KT])
        pi = sb("pi", [P, 2, KT], I32)
        eg = sb("eg", [P, 2, KT])
        gate = sb("gate", [P, KT])
        iota_e = sb("iota_e", [P, KT, NE])
        valid = sb("valid", [P, KT, NE])
        trash = sb("trash", [P, 2, KT])
        tok = sb("tok", [P, KT])
        run = keep["run"]

        S = ctx.enter_context(nc.psum_tensor("S", [P, 4, 512], F32))
        O = ctx.enter_context(nc.psum_tensor("O", [P, 3, 512], F32))
        AUX = ctx.enter_context(nc.psum_tensor("AUX", [P, 512], F32))

        s_const = sem("s_const")
        s_zero = sem("s_zero")
        s_wo = sem("s_wo")
        s_w = [sem("s_w0"), sem("s_w1")]
        s_h = sem("s_h")
        s_dve = sem("s_dve")
        s_xn = sem("s_xn")
        s_xt = sem("s_xt")
        s_xnT = sem("s_xnT")
        s_aux = sem("s_aux")
        s_hi = sem("s_hi")
        s_lo = sem("s_lo")
        s_evac = sem("s_evac")
        s_qd = sem("s_qd")
        s_kd = sem("s_kd")
        s_qk = sem("s_qk")
        s_th = sem("s_th")
        s_ex = sem("s_ex")
        s_mask = sem("s_mask")
        s_sum = sem("s_sum")
        s_psum = sem("s_psum")
        s_pv = sem("s_pv")
        s_norm = sem("s_norm")
        s_y = sem("s_y")
        s_h2 = sem("s_h2")
        s_lg = sem("s_lg")
        s_ge = sem("s_ge")
        s_cc = sem("s_cc")
        s_rank = sem("s_rank")
        s_pos = sem("s_pos")
        s_sc = sem("s_sc")
        s_hs = sem("s_hs")
        s_apart = sem("s_apart")

        def apart(eng):
            eng.sem_inc(s_apart, 1)

        def add_to_sums(ops, eng, j, n, signal, first_done):
            s = SLOTS[n]
            (h0, _, q0), (h1, _, _) = s["halves"]
            w, tail = s["n"], s.get("tail", 0)
            pr = PR[:, (j * NS + n) % PRING, 0:2 * w]
            if h0 == h1:
                dst, src = SUM[:, h0, q0:q0 + 2 * w], pr
            else:
                pr = pr.rearrange("p (h q) -> p h q", h=2)
                dst, src = SUM[:, :, q0:q0 + w - tail], pr[:, :, 0:w - tail]
            ops.tensor_tensor(dst, dst, src, ALU.add).then_inc(signal, 1)
            if tail:
                eng.wait_ge(signal, first_done)
                dst = SUM[0:1, :, T - 1:TQ]
                ops.tensor_tensor(dst, dst, pr[0:1, :, w - tail:w], ALU.add).then_inc(signal, 1)

        def pairs(engine, b, pair):
            base = b * AUX_BATCH
            pair(0, 0, base + len(PROJ), b * (PAIRS // 2) + 1, "first")
            with engine.Fori(0, PAIRS // 2 - 1) as pp:
                for k in range(2):
                    pair(2 * pp + 1 + k, 1 - k, base + AUX_FIRST + (2 * pp + k) * len(JOB_AT),
                         b * (PAIRS // 2) + pp + 2, "mid")
            pair(PAIRS - 1, 1, base + AUX_LAST, None, "last")

        block = ctx.enter_context(nc.Block())

        @block.sync
        def _(sp):
            sp.dma_start(WO[:], wot).then_inc(s_wo, 16)
            sp.dma_start(R[:], router).then_inc(s_wo, 16)
            for j in range(2):
                sp.dma_start(W[j][:], wqkv[j]).then_inc(s_w[j], 16)
            sp.wait_ge(s_zero, 1)

            def spread(j, g):
                def half(dst, src, s):
                    sp.dma_start(dst.bitcast(F32), src.bitcast(F32)).then_inc(s, 16)

                sp.wait_ge(s_lo, 2 + 6 * g + 3)
                for h in range(2):
                    for o in range(2):
                        half(q4[j][64 * o:64 * o + 64, h], qN[64 * h:64 * h + 64], s_qd)
                sp.wait_ge(s_lo, 2 + 6 * g + 6)
                for h in range(2):
                    for part in range(2):
                        half(kS[j][64 * part:64 * part + 64, h, 0:TQ],
                             kN[64 * h:64 * h + 64, part], s_kd)

            with sp.Fori(0, B) as b:
                sp.dma_start(H[0:1, 0], cls).then_inc(s_h, 16)
                sp.dma_start(H[1:P, 0], x[b, 0:P - 1]).then_inc(s_h, 16)
                sp.dma_start(H[:, 1:KT - 1],
                             x[b, P - 1:X - 1].rearrange("(t p) d -> p t d", p=P)).then_inc(s_h, 16)
                sp.dma_start(H[0:1, KT - 1], x[b, X - 1:X]).then_inc(s_h, 16)
                spread(0, b * PAIRS)

                def pair(p, j, done, loads, kind):
                    sp.wait_ge(s_aux, done)
                    apart(sp)
                    sp.dma_start(W[j][:], wqkv[p + 2]).then_inc(s_w[j], 16)
                    if kind != "last":
                        spread(1 - j, b * PAIRS + p + 1)

                pairs(sp, b, pair)
                sp.wait_ge(s_h2, (b + 1) * KT)
                sp.dma_start(out[bass.ds(b * T, X)].rearrange("(t p) d -> p t d", p=P),
                             H[:, 0:KT - 1]).then_inc(s_hs, 16)
                sp.dma_start(out[bass.ds(b * T + X, 1)], H[0:1, KT - 1]).then_inc(s_hs, 16)
                sp.wait_ge(s_hs, (b + 1) * 32)
                apart(sp)
                sp.wait_ge(s_xn, 2 * b + 2)
                apart(sp)
            sp.wait_ge(s_hs, B * 32)
            for j in range(2):
                sp.wait_ge(s_w[j], 16 * (B * PAIRS // 2 + 1))

        @block.gpsimd
        def _(pool):
            nc.gpsimd.memset(ones[:], 1.0).then_inc(s_const, 1)
            pool.wait_ge(s_const, 1)
            nc.gpsimd.affine_select(out=ident[:], in_=ones[:], compare_op=ALU.is_equal, fill=0.0,
                                    base=0, pattern=[[-1, P]], channel_multiplier=1).then_inc(s_const, 1)
            nc.gpsimd.affine_select(out=upper[:], in_=ones[:], compare_op=ALU.is_gt, fill=0.0,
                                    base=0, pattern=[[1, P]], channel_multiplier=-1).then_inc(s_const, 1)
            nc.gpsimd.iota(iota_e[:], pattern=[[0, KT], [1, NE]], base=0, channel_multiplier=0,
                           allow_small_or_imprecise_dtypes=True).then_inc(s_const, 1)
            nc.gpsimd.memset(valid[:], 1.0).then_inc(s_const, 1)
            pool.wait_ge(s_const, 5)
            nc.gpsimd.affine_select(out=valid[:, KT - 1], in_=valid[:, KT - 1], compare_op=ALU.is_ge,
                                    fill=0.0, base=0, pattern=[[0, NE]],
                                    channel_multiplier=-1).then_inc(s_const, 1)
            nc.gpsimd.iota(trash[:], pattern=[[P, 2], [0, KT]], base=TRASH, channel_multiplier=1,
                           allow_small_or_imprecise_dtypes=True).then_inc(s_const, 1)
            pool.wait_ge(s_const, 7)
            nc.gpsimd.memset(trash[:, :, 0:KT - 1], 0.0).then_inc(s_const, 1)
            nc.gpsimd.memset(trash[0:1, :, KT - 1:KT], 0.0).then_inc(s_const, 1)
            nc.gpsimd.iota(tok[:], pattern=[[P, KT]], base=0, channel_multiplier=1,
                           allow_small_or_imprecise_dtypes=True).then_inc(s_const, 1)

            pool.sem_inc(s_lo, 2)
            pool.sem_inc(s_psum, PSUMS)

            def mask(g, j, n):
                if n not in DIAG:
                    return
                s = SLOTS[n]
                h0, h1 = s["halves"]
                pool.wait_ge(s_ex, 2 + g * NS + n + 1)
                apart(pool)
                pr = PR[:, (j * NS + n) % PRING, 0:2 * s["n"]]
                if h0[0] == h1[0]:
                    v, pat = pr[:, 0:P], [[1, P]]
                else:
                    v = pr.rearrange("p (h q) -> p h q", h=2)[:, :, 0:P]
                    pat = [[0, 2], [1, P]]
                nc.gpsimd.affine_select(out=v, in_=v, compare_op=ALU.is_ge, fill=0.0, base=0,
                                        pattern=pat, channel_multiplier=-1).then_inc(s_mask, 1)

            def sums(g, j, n):
                if n < DSUMS:
                    return
                if n == DSUMS:
                    pool.wait_ge(s_sum, DSUMS + (g + 1) * DSUMS)
                pool.wait_ge(s_mask, g * len(DIAG) + masks_through(n))
                if n > DSUMS:
                    pool.wait_ge(s_psum, PSUMS + g * PSUMS + pool_sums_through(n - 1))
                add_to_sums(nc.gpsimd, pool, j, n, s_psum, PSUMS + g * PSUMS + pool_sums_through(n - 1) + 1)

            def low(g, what, c, done):
                i = 3 * "qk".index(what) + c
                dst = (qN, kN)["qk".index(what)]
                cols = slice(c * QC, c * QC + QW[c])
                pool.wait_ge(s_hi, 6 * g + i + 1)
                nc.gpsimd.tensor_tensor(dst[:, 1, cols], raw[:, i % 2, 0:QW[c]], dst[:, 0, cols].bitcast(F32),
                                        ALU.subtract).then_inc(s_lo, 1)

            def slot(g, j, n):
                mask(g, j, n)
                sums(g, j, n)

            with pool.Fori(0, B) as b:
                for what, c in PROJ[:6]:
                    low(b * PAIRS, what, c, None)

                def pair(p, j, done, loads, kind):
                    g = b * PAIRS + p
                    for n in range(NS):
                        if n >= 1:
                            slot(g, j, n - 1)
                        elif kind != "first":
                            slot(g - 1, 1 - j, NS - 1)
                        if has_job(n - 1, kind) and JOB_AT[n - 1][0] in "qk":
                            low(g + 1, *JOB_AT[n - 1], None)

                pairs(pool, b, pair)
                slot(b * PAIRS + PAIRS - 1, 1, NS - 1)
                pool.wait_ge(s_pos, b + 1)
                apart(pool)
                for t in range(KT):
                    for k in range(2):
                        nc.gpsimd.indirect_dma_start(
                            xs, bass.IndirectOffsetOnAxis(pi[:, k, t:t + 1], 0),
                            XN[:, t], None).then_inc(s_sc, 16)
            pool.wait_ge(s_sc, B * KT * 2 * 16)

        @block.scalar
        def _(act):
            act.sem_inc(s_th, 2)
            act.sem_inc(s_ex, 2)

            def hi(g, what, c, done):
                k = "qk".index(what)
                act.wait_ge(s_evac, 1 + done + 1)
                nc.scalar.copy((qN, kN)[k][:, 0, c * QC:c * QC + QW[c]],
                               raw[:, (3 * k + c) % 2, 0:QW[c]]).then_inc(s_hi, 1)

            def tanh(g, j, n):
                s = SLOTS[n]
                act.wait_ge(s_qk, g * NS + n + 1)
                act.wait_ge(s_ex, 2 + g * NS + n - THRING + 1)
                nc.scalar.activation(
                    TH[:, (j * NS + n) % THRING, 0:2 * s["n"]].rearrange("p (h q) -> p h q", h=2),
                    S[:, 2 * (n % 2):2 * (n % 2) + 2, 0:s["n"]], ACT.Tanh,
                    scale=SCALE / CLAMP).then_inc(s_th, 1)

            def exp(g, j, n):
                s = SLOTS[n]
                act.wait_ge(s_th, 2 + g * NS + n + 1)
                m, ago = (n - PRING, 0) if n >= PRING else (n - PRING + NS, 1)
                act.wait_ge(s_pv, (1 - ago) * NU + g * NU + UNIT_OF[m] + 1)
                if m < DSUMS:
                    act.wait_ge(s_sum, (1 - ago) * DSUMS + g * DSUMS + m + 1)
                else:
                    act.wait_ge(s_psum, (1 - ago) * PSUMS + g * PSUMS + pool_sums_through(m))
                nc.scalar.activation(PR[:, (j * NS + n) % PRING, 0:2 * s["n"]],
                                     TH[:, (j * NS + n) % THRING, 0:2 * s["n"]], ACT.Exp,
                                     scale=CLAMP).then_inc(s_ex, 1)

            with act.Fori(0, B) as b:
                for jj, (what, c) in enumerate(PROJ[:6]):
                    hi(b * PAIRS, what, c, b * AUX_BATCH + jj)

                def pair(p, j, done, loads, kind):
                    g = b * PAIRS + p
                    for n in range(NS):
                        if has_job(n - 1, kind) and JOB_AT[n - 1][0] in "qk":
                            hi(g + 1, *JOB_AT[n - 1], done + jobs_before(n - 1, kind))
                        tanh(g, j, n)
                        if n >= 1:
                            exp(g, j, n - 1)
                        elif kind != "first":
                            exp(g - 1, 1 - j, NS - 1)

                pairs(act, b, pair)
                exp(b * PAIRS + PAIRS - 1, 1, NS - 1)
                act.wait_ge(s_ge, 2 * b + 1)
                nc.scalar.activation(eg[:, 0], eg[:, 1], ACT.Exp).then_inc(s_ge, 1)

        @block.tensor
        def _(pe):
            def qk(g, j, n):
                s = SLOTS[n]
                if n == 0:
                    pe.wait_ge(s_qd, 64 * (g + 1))
                    pe.wait_ge(s_kd, 64 * (g + 1))
                pe.wait_ge(s_th, g * NS + n + 1)
                tail = s.get("tail", 0)
                for k, (h, i, q0) in enumerate(s["halves"]):
                    out = S[:, 2 * (n % 2) + k]
                    runs = [(i, q0, 0, s["n"] - tail)]
                    if tail:
                        runs.append((i + 1, T - 1, s["n"] - tail, s["n"]))
                    for i_, q, a, e in runs:
                        for part in range(2):
                            mm = nc.tensor.matmul(out[:, a:e], kS[j][:, h, P * i_:P * i_ + P],
                                                  q4[j][:, h, part, q:q + e - a],
                                                  start=(part == 0), stop=(part == 1))
                mm.then_inc(s_qk, 1)

            def pv(g, j, u):
                n = max(UNITS[u])
                if u == 0:
                    pe.wait_ge(s_norm, 1 + 3 * g)
                    pe.wait_ge(s_ex, 2 + g * NS + n + 1)
                pe.wait_ge(s_mask, g * len(DIAG) + masks_through(n))
                for n_, col, h, i, c, a, e in pv_pieces(u):
                    K = 1 if i == KT - 1 else P
                    last = i == CHUNK_LAST[c]
                    mm = nc.tensor.matmul(O[64 * h:64 * h + 64, c, a - c * QC:e - c * QC],
                                          V[j][0:K, i, 64 * h:64 * h + 64],
                                          PR[0:K, (j * NS + n_) % PRING, col:col + e - a],
                                          start=(i == 0), stop=last, skip_group_check=True)
                mm.then_inc(s_pv, 1)

            CHUNK_LAST = [2, 5, KT - 1]

            def job(kind, c, j, g, loads, done):
                pe.wait_ge(s_evac, 1 + done)
                if kind in "qk":
                    w = "qk".index(kind)
                    if kind == "q" and c == 0:
                        pe.wait_ge(s_w[j], 16 * loads)
                    for ci in range(C):
                        mm = nc.tensor.matmul(AUX[:, 0:QW[c]], W[j][:, w, ci],
                                              xnT[:, ci, c * QC:c * QC + QW[c]],
                                              start=(ci == 0), stop=(ci == C - 1))
                elif kind == "v":
                    for t in range(3):
                        for ci in range(C):
                            tok = P * (3 * c + t)
                            mm = nc.tensor.matmul(AUX[:, P * t:P * t + P], xnT[:, ci, tok:tok + P],
                                                  W[j][:, 2, ci], start=(ci == 0), stop=(ci == C - 1))
                else:
                    m = CHUNK_SLOT[c]
                    if m < DSUMS:
                        pe.wait_ge(s_sum, DSUMS + g * DSUMS + m + 1)
                    else:
                        pe.wait_ge(s_psum, PSUMS + g * PSUMS + pool_sums_through(m))
                    for h in range(2):
                        mm = nc.tensor.matmul(AUX[64 * h:64 * h + 64, 0:QW[c]], ones[:, 0:64],
                                              SUM[:, h, c * QC:c * QC + QW[c]],
                                              start=True, stop=True, skip_group_check=True)
                mm.then_inc(s_aux, 1)

            def transposes(n):
                pe.wait_ge(s_xn, n)
                for ci in range(C):
                    for t in range(KT):
                        out = (S[:, 2 * ci + t // 4, P * (t % 4):P * (t % 4) + P] if t < KT - 1
                               else O[:, 0, P * ci:P * ci + P])
                        mm = nc.tensor.transpose(out, XN[:, t, P * ci:P * ci + P], ident[:])
                mm.then_inc(s_xt, 1)

            pe.sem_inc(s_pv, NU)
            pe.wait_ge(s_const, 10)
            pe.wait_ge(s_wo, 32)
            with pe.Fori(0, B) as b:
                transposes(2 * b + 1)
                pe.wait_ge(s_xnT, 2 * b + 1)
                for jj, (what, c) in enumerate(PROJ):
                    job(what, c, 0, None, b * (PAIRS // 2) + 1, b * AUX_BATCH + jj)

                def pair(p, j, done, loads, kind):
                    g = b * PAIRS + p
                    for n in range(NS):
                        qk(g, j, n)
                        if n in UNIT_AT:
                            u, off = UNIT_AT[n]
                            if off == 0:
                                pv(g, j, u)
                            elif kind != "first":
                                pv(g - 1, 1 - j, u)
                        if has_job(n, kind):
                            what, c = JOB_AT[n]
                            at = done + jobs_before(n, kind)
                            if what != "den":
                                job(what, c, 1 - j, None, loads, at)
                            elif c == 0:
                                job(what, c, j, g, None, at)
                            else:
                                job(what, c, 1 - j, g - 1, None, at)

                pairs(pe, b, pair)
                g = b * PAIRS + PAIRS - 1
                pv(g, 1, 5)
                job("den", 1, 1, g, None, (b + 1) * AUX_BATCH - 2)
                pv(g, 1, 6)
                pv(g, 1, 7)
                job("den", 2, 1, g, None, (b + 1) * AUX_BATCH - 1)
                pe.wait_ge(s_th, 2 + (b + 1) * PAIRS * NS)
                pe.wait_ge(s_norm, 1 + 3 * PAIRS * (b + 1))
                for t in range(KT):
                    if t >= 4:
                        pe.wait_ge(s_h2, b * KT + t - 3)
                    m = P if t < KT - 1 else 1
                    for p in range(PAIRS):
                        mm = nc.tensor.matmul(S[0:m, t % 4, 0:D], OT[:, p, P * t:P * t + m], WO[:, p],
                                              start=(p == 0), stop=(p == PAIRS - 1))
                    mm.then_inc(s_y, 1)
                pe.wait_ge(s_h2, (b + 1) * KT)
                transposes(2 * b + 2)
                pe.wait_ge(s_xnT, 2 * b + 2)
                for t in range(KT):
                    for ci in range(C):
                        mm = nc.tensor.matmul(O[:, 1, NE * t:NE * t + NE], xnT[:, ci, P * t:P * t + P],
                                              R[:, ci], start=(ci == 0), stop=(ci == C - 1))
                mm.then_inc(s_lg, 1)
                pe.wait_ge(s_cc, b + 1)
                nc.tensor.matmul(O[:, 2, 0:KT * NE], upper[:], CC[:].rearrange("p t e -> p (t e)"),
                                 start=True, stop=True)
                nc.tensor.matmul(O[:, 2, 128:128 + KT * NE], ones[:], CC[:].rearrange("p t e -> p (t e)"),
                                 start=True, stop=True).then_inc(s_rank, 1)
                pe.wait_ge(s_pos, b + 1)

        @block.vector
        def _(dve):
            v = nc.vector
            zeros = [H[:, KT - 1], run[:], ]
            for j in range(2):
                zeros.append(kS[j][:, :, T:TP].bitcast(F32))
            for z in zeros:
                v.memset(z, 0.0).then_inc(s_dve, 1)
            dve.wait_ge(s_dve, len(zeros))
            dve.sem_inc(s_zero, 1)
            dve.sem_inc(s_sum, DSUMS)
            dve.sem_inc(s_evac, 1)
            dve.sem_inc(s_norm, 1)
            dve.wait_ge(s_const, 10)
            count = [0]

            def link(ins):
                count[0] += 1
                ins.then_inc(s_dve, 1)
                dve.wait_ge(s_dve, chain_base + count[0])

            def layernorm(b, n):
                for t in range(KT):
                    ins = v.bn_stats(st[:, t], H[:, t])
                    if t < KT - 1:
                        ins.then_inc(s_dve, 1)
                        count[0] += 1
                link(ins)
                apart(dve)
                for t in range(KT):
                    ins = v.bn_aggr(mv[:, t], st[:, t])
                    if t < KT - 1:
                        ins.then_inc(s_dve, 1)
                        count[0] += 1
                link(ins)
                rsqrt_steps(v, link, mv[:, :, 1], rs, vh, nt, LN1_EPS)
                for t in range(KT):
                    ins = v.tensor_scalar(XN[:, t, 0:D], H[:, t], mv[:, t, 0:1], rs[:, t:t + 1],
                                          ALU.subtract, ALU.mult)
                    ins.then_inc(s_dve, 1)
                    count[0] += 1
                dve.wait_ge(s_dve, chain_base + count[0])
                dve.sem_inc(s_xn, 1)

            def turned(b, n):
                dve.wait_ge(s_xt, n)
                v.tensor_copy(xnT[:, :, 0:X].rearrange("p c (k q) -> p c k q", k=2),
                              S[:].rearrange("p (c k) q -> p c k q", c=C)).then_inc(s_dve, 1)
                v.tensor_copy(xnT[:, :, X:TP], O[:, 0, 0:2 * P].rearrange("p (c q) -> p c q", c=C)).then_inc(s_dve, 1)
                count[0] += 2
                dve.wait_ge(s_dve, chain_base + count[0])
                dve.sem_inc(s_xnT, 1)

            def read_out(what, c, j, g, done):
                dve.wait_ge(s_aux, done + 1)
                if what in "qk":
                    i = 3 * "qk".index(what) + c
                    dve.wait_ge(s_lo, 6 * g + i + 1)
                    v.tensor_copy(raw[:, i % 2, 0:QW[c]], AUX[:, 0:QW[c]]).then_inc(s_evac, 1)
                else:
                    v.tensor_copy(V[j][:, 3 * c:3 * c + 3],
                                  AUX[:, 0:3 * P].rearrange("p (t f) -> p t f", t=3)).then_inc(s_evac, 1)

            def sums(g, j, n, done):
                if n in DIAG:
                    dve.wait_ge(s_mask, g * len(DIAG) + masks_through(n))
                else:
                    dve.wait_ge(s_ex, 2 + g * NS + n + 1)
                (h0, i, q0), (h1, _, q1) = SLOTS[n]["halves"]
                w = SLOTS[n]["n"]
                if i == 0:
                    dve.wait_ge(s_aux, done)
                    pr = PR[:, (j * NS + n) % PRING, 0:2 * w]
                    if h0 == h1:
                        dst = SUM[:, h0, q0:q0 + 2 * w]
                    else:
                        pr, dst = pr.rearrange("p (h q) -> p h q", h=2), SUM[:, :, q0:q0 + w]
                    v.tensor_copy(dst, pr).then_inc(s_sum, 1)
                else:
                    dve.wait_ge(s_sum, DSUMS + g * DSUMS + max(n - 1, 3))
                    add_to_sums(v, dve, j, n, s_sum, None)

            def normalise(g, p, c, done):
                dve.wait_ge(s_aux, done + 1)
                dve.wait_ge(s_norm, 1 + 3 * g + c)
                v.reciprocal(RC[:, 0:QW[c]], AUX[:, 0:QW[c]]).then_inc(s_evac, 1)
                dve.wait_ge(s_evac, 1 + done + 1)
                dve.wait_ge(s_pv, NU + g * NU + CHUNK_UNIT[c] + 1)
                v.tensor_tensor(OT[:, bass.ds(p, 1), c * QC:c * QC + QW[c]].rearrange("p a q -> p (a q)"),
                                O[:, c, 0:QW[c]], RC[:, 0:QW[c]], ALU.mult).then_inc(s_norm, 1)

            with dve.Fori(0, B) as b:
                chain_base = len(zeros) + b * CHAIN
                count[0] = 0
                dve.wait_ge(s_h, 64 * (b + 1))
                layernorm(b, 2 * b + 1)
                turned(b, 2 * b + 1)
                for jj, (what, c) in enumerate(PROJ):
                    read_out(what, c, 0, b * PAIRS, b * AUX_BATCH + jj)

                def pair(p, j, done, loads, kind):
                    g = b * PAIRS + p
                    for n in range(NS):
                        m = n - 2
                        if 0 <= m < DSUMS:
                            sums(g, j, m, done + jobs_before(2 if m < 2 else 4, kind) if kind != "first" else done)
                        if has_job(n, kind):
                            what, c = JOB_AT[n]
                            at = done + jobs_before(n, kind)
                            if what != "den":
                                read_out(what, c, 1 - j, g + 1, at)
                            elif c == 0:
                                normalise(g, p, c, at)
                            else:
                                normalise(g - 1, p - 1, c, at)

                pairs(dve, b, pair)
                for c in (1, 2):
                    normalise(b * PAIRS + PAIRS - 1, PAIRS - 1, c, (b + 1) * AUX_BATCH - 3 + c)
                for t in range(KT):
                    m = P if t < KT - 1 else 1
                    dve.wait_ge(s_y, b * KT + t + 1)
                    v.tensor_tensor(H[0:m, t], H[0:m, t], S[0:m, t % 4, 0:D], ALU.add).then_inc(s_h2, 1)
                dve.wait_ge(s_h2, (b + 1) * KT)
                layernorm(b, 2 * b + 2)
                turned(b, 2 * b + 2)
                dve.wait_ge(s_lg, b + 1)
                link(v.tensor_copy(lg[:].rearrange("p t e -> p (t e)"), O[:, 1, 0:KT * NE]))
                apart(dve)
                for t in range(KT):
                    ins = v.max(top[:, t], lg[:, t])
                    ins.then_inc(s_dve, 1)
                    count[0] += 1
                dve.wait_ge(s_dve, chain_base + count[0])
                apart(dve)
                for t in range(KT):
                    ins = v.max_index(ti[:, t], top[:, t], lg[:, t])
                    ins.then_inc(s_dve, 1)
                    count[0] += 1
                dve.wait_ge(s_dve, chain_base + count[0])
                v.tensor_tensor(eg[:, 1], top[:, :, 1], top[:, :, 0], ALU.subtract).then_inc(s_ge, 1)
                link(v.tensor_copy(tf[:], ti[:, :, 0:2]))
                for k in range(2):
                    link(v.tensor_tensor(M[:, k], iota_e[:], tf[:, :, k:k + 1].to_broadcast([P, KT, NE]),
                                         ALU.is_equal))
                for k in range(2):
                    link(v.tensor_tensor(M[:, k], M[:, k], valid[:], ALU.mult))
                v.tensor_tensor(CC[:], M[:, 0], M[:, 1], ALU.add).then_inc(s_cc, 1)
                dve.wait_ge(s_ge, 2 * b + 2)
                link(v.tensor_scalar(eg[:, 1], eg[:, 0], 1.0, None, ALU.add))
                link(v.reciprocal(gate[:], eg[:, 1]))
                link(v.tensor_tensor(XN[:, :, G2], gate[:], eg[:, 0], ALU.mult))
                link(v.tensor_tensor(XN[:, :, DG], gate[:], XN[:, :, G2], ALU.subtract))
                link(v.tensor_copy(XN[:, :, E1], tf[:, :, 0]))
                link(v.tensor_copy(XN[:, :, TOK], tok[:]))
                link(v.tensor_scalar(tok[:], tok[:], float(T), None, ALU.add))
                dve.wait_ge(s_rank, b + 1)
                for t in range(KT):
                    link(v.tensor_tensor(rank[:, t], O[:, 2, NE * t:NE * t + NE], run[:], ALU.add))
                    link(v.tensor_tensor(run[:], run[:], O[:, 2, 128 + NE * t:128 + NE * t + NE], ALU.add))
                link(v.scalar_tensor_tensor(out=rank[:], in0=iota_e[:], scalar=float(REGION),
                                            in1=rank[:], op0=ALU.mult, op1=ALU.add))
                for k in range(2):
                    link(v.tensor_tensor(mr[:, k], M[:, k], rank[:], ALU.mult))
                link(v.tensor_reduce(pf[:], mr[:], AX.X, ALU.add))
                link(v.tensor_tensor(pf[:], pf[:], trash[:], ALU.add))
                link(v.tensor_copy(pi[:], pf[:]))
                dve.sem_inc(s_pos, 1)
                dve.wait_ge(s_sc, (b + 1) * KT * 2 * 16)
                apart(dve)
                assert count[0] == CHAIN, count[0]




def rsqrt_steps(v, link, var, y, h, t, eps):
    link(v.tensor_scalar(h[:], var, eps, None, ALU.add))
    link(v.tensor_scalar(t[:].bitcast(I32), h[:].bitcast(I32), 1, None, ALU.arith_shift_right))
    link(v.tensor_scalar(y[:].bitcast(I32), t[:].bitcast(I32), -1.0, float(0x5F3759DF), ALU.mult, ALU.add))
    link(v.tensor_scalar(h[:], h[:], -0.5, None, ALU.mult))
    for _ in range(3):
        link(v.tensor_tensor(t[:], y[:], y[:], ALU.mult))
        link(v.tensor_tensor(t[:], t[:], h[:], ALU.mult))
        link(v.scalar_tensor_tensor(out=y[:], in0=t[:], scalar=1.5, in1=y[:], op0=ALU.add, op1=ALU.mult))


def experts(nc, io, xs, out, keep):
    w1, b1, w2, bc = io["w1"], io["b1"], io["w2"], io["bc"]
    run = keep["run"]
    with ExitStack() as ctx:
        def sb(name, shape, dt=F32):
            return ctx.enter_context(nc.sbuf_tensor(name, shape, dt))

        def sem(name):
            return ctx.enter_context(nc.semaphore(name))

        def pair_of(name, shape, dt=F32):
            return [sb(f"{name}{j}", shape, dt) for j in range(2)]

        def sems(name):
            return [sem(f"{name}{j}") for j in range(2)]

        ident = sb("ident2", [P, P])
        ones = sb("ones2", [P, P])
        fill = sb("fill", [P, TS, ROW])
        thr = sb("thr", [P, NE, MAXT])
        cmp = sb("cmp", [P, NE, MAXT])
        nt = sb("ntiles", [P, NE])
        ce = sb("ce", [P, NE])
        ci = sb("ci", [P, NE])
        tid = sb("tid", [P, NTILE, NE])
        eid = sb("eid", [P, NTILE, NE])
        a = sb("a", [P, NTILE, NE])
        z = sb("z", [P, NTILE, NE])
        EF = sb("EF", [P, NTILE])
        SF = sb("SF", [P, NTILE])
        EI = sb("EI", [P, NTILE], I32)
        SI = sb("SI", [P, NTILE], I32)
        zf = sb("zf", [P, NE])
        ZI = sb("ZI", [P, NE], I32)
        eb = sb("eb", [P, NE])

        XR = pair_of("XR", [P, TS, ROW])
        W1s = sb("W1s", [P, C * F])
        W2s = sb("W2s", [P, FM * D])
        W1 = pair_of("W1_", [P, 2, C * F], F32R)
        W2 = pair_of("W2_", [P, 2, FM * D], F32R)
        B1 = pair_of("B1_", [P, FM])
        BC = pair_of("BC_", [P, 3, D])
        xT = pair_of("xT_", [P, 2, C, TT], F32R)
        h32 = sb("h32", [P, HRING, TT])
        hT = sb("hT", [P, 2, FM, TT], F32R)
        XB = sb("XB", [P, TS, D])
        RES = sb("RES", [P, TS, D])
        NRM = sb("NRM", [P, TS, D])
        GM = sb("GM", [P, TS, D])
        OUT = pair_of("OUT_", [P, TS, D])
        IDX = pair_of("IDX_", [P, TS], I32)
        st = sb("st2", [P, TS, 6])
        mv = sb("mv2", [P, TS, 2])
        rs = sb("rs2", [P, TS])
        vh = sb("vh2", [P, TS])
        tt_ = sb("tt2", [P, TS])
        g = sb("g2", [P, TS])
        rg = sb("rg2", [P, TS])

        H1 = ctx.enter_context(nc.psum_tensor("H1", [P, 4, 512], F32))
        Y2 = ctx.enter_context(nc.psum_tensor("Y2", [P, TS, 512], F32))
        XP = ctx.enter_context(nc.psum_tensor("XP", [P, 512], F32))

        s_const = sem("e_const")
        s_list = sem("e_list")
        s_fill = sem("e_fill")
        s_x = sems("e_x")
        s_bc = sems("e_bc")
        s_w1s = sem("e_w1s")
        s_w2s = sem("e_w2s")
        s_wh = sem("e_wh")
        s_w1 = sem("e_w1")
        s_w2 = sem("e_w2")
        s_xp = sem("e_xp")
        s_xh = sem("e_xh")
        s_xT = sem("e_xT")
        s_m1 = sem("e_m1")
        s_ge = sem("e_ge")
        s_hl = sem("e_hl")
        s_m2 = sem("e_m2")
        s_xb = sem("e_xb")
        s_res = sem("e_res")
        s_ch = sem("e_ch")
        s_nrm = sem("e_nrm")
        s_gm = sem("e_gm")
        s_out = sem("e_out")
        s_apart = sem("e_apart")
        s_add = sem("e_add")
        s_clear = sem("e_clear")

        def apart(eng):
            eng.sem_inc(s_apart, 1)

        block = ctx.enter_context(nc.Block())
        HALF = NTILE // 2
        assert NTILE % 2 == 1
        LIST = 31
        WC = C * F // 4
        assert C * F == FM * D

        @block.sync
        def _(sp):
            sp.wait_ge(s_const, 7)
            sp.dma_start(xs[SPARE:SPARE + TT].rearrange("(t p) d -> p t d", p=P), fill[:]).then_inc(s_fill, 16)
            sp.wait_ge(s_list, LIST)
            with sp.Fori(0, NE) as e:
                row = sp.value_load(ZI[0:1, bass.ds(e, 1)], min_val=0, max_val=SPARE - TT)
                sp.dma_start(xs[bass.ds(row, TT)].rearrange("(t p) d -> p t d", p=P), fill[:]).then_inc(s_fill, 16)

            def weights(t, first=False):
                if not first:
                    sp.wait_ge(s_w1, 8 * t)
                    apart(sp)
                e = sp.value_load(EI[0:1, bass.ds(t, 1)], min_val=0, max_val=NE - 1)
                sp.dma_start(W1s[:].rearrange("p (c f) -> p c f", c=C),
                             w1[bass.ds(e, 1)].rearrange("a (c p) f -> p (a c) f", p=P)).then_inc(s_w1s, 16)
                if not first:
                    sp.wait_ge(s_w2, 4 * t)
                sp.dma_start(W2s[:].rearrange("p (m d) -> p m d", m=FM),
                             w2[bass.ds(e, 1)].rearrange("a (m p) d -> p (a m) d", p=P)).then_inc(s_w2s, 16)

            def rows(t, j, first=False):
                if not first:
                    sp.wait_ge(s_res, t)
                    apart(sp)
                row = sp.value_load(SI[0:1, bass.ds(t, 1)], min_val=0, max_val=SPARE)
                e = sp.value_load(EI[0:1, bass.ds(t, 1)], min_val=0, max_val=NE - 1)
                sp.dma_start(XR[j][:], xs[bass.ds(row, TT)].rearrange("(t p) d -> p t d", p=P)).then_inc(s_x[j], 16)
                sp.dma_start(B1[j][:], b1[bass.ds(e, 1)].rearrange("a p m -> p (a m)")).then_inc(s_x[j], 16)
                if not first:
                    sp.wait_ge(s_out, t)
                sp.dma_start(BC[j][:], bc[bass.ds(e, 1)].to_broadcast([P, 3, D])).then_inc(s_bc[j], 16)

            weights(0, first=True)
            sp.wait_ge(s_fill, 16 * (1 + NE))
            rows(0, 0, first=True)
            rows(1, 1, first=True)
            weights(1)
            weights(2)
            with sp.Fori(1, HALF) as k:
                rows(2 * k, 0)
                weights(2 * k + 1)
                rows(2 * k + 1, 1)
                weights(2 * k + 2)
            rows(NTILE - 1, 0)

        @block.gpsimd
        def _(pool):
            nc.gpsimd.memset(ones[:], 1.0).then_inc(s_const, 1)
            nc.gpsimd.memset(fill[:], 0.0).then_inc(s_const, 1)
            pool.wait_ge(s_const, 2)
            nc.gpsimd.affine_select(out=ident[:], in_=ones[:], compare_op=ALU.is_equal, fill=0.0,
                                    base=0, pattern=[[-1, P]], channel_multiplier=1).then_inc(s_const, 1)
            nc.gpsimd.iota(fill[:, :, TOK], pattern=[[P, TS]], base=B * T, channel_multiplier=1,
                           allow_small_or_imprecise_dtypes=True).then_inc(s_const, 1)
            nc.gpsimd.iota(thr[:], pattern=[[0, NE], [TT, MAXT]], base=0, channel_multiplier=0,
                           allow_small_or_imprecise_dtypes=True).then_inc(s_const, 1)
            nc.gpsimd.iota(tid[:], pattern=[[1, NTILE], [0, NE]], base=0, channel_multiplier=0,
                           allow_small_or_imprecise_dtypes=True).then_inc(s_const, 1)
            nc.gpsimd.iota(eid[:], pattern=[[0, NTILE], [REGION, NE]], base=0, channel_multiplier=0,
                           allow_small_or_imprecise_dtypes=True).then_inc(s_const, 1)
            pool.wait_ge(s_const, 7)
            nc.gpsimd.dma_start(out[B * T:B * T + TT].rearrange("(t p) d -> p t d", p=P),
                                fill[:, :, 0:D]).then_inc(s_add, 16)
            pool.sem_inc(s_gm, 1)
            pool.sem_inc(s_clear, 1)

            def bias(t, j, k):
                pool.wait_ge(s_x[j], 32 * (k + 1))
                pool.wait_ge(s_bc[j], 16 * (k + 1))
                pool.wait_ge(s_res, 1 + t)
                nc.gpsimd.tensor_tensor(XB[:], XR[j][:, :, 0:D], BC[j][:, 0:1].to_broadcast([P, TS, D]),
                                        ALU.add).then_inc(s_xb, 1)

            def low(t, j):
                for q in range(4):
                    cols = slice(q * WC, (q + 1) * WC)
                    pool.wait_ge(s_wh, 8 * t + 4 + q + 1)
                    nc.gpsimd.tensor_tensor(W2[j][:, 1, cols], W2s[:, cols], W2[j][:, 0, cols].bitcast(F32),
                                            ALU.subtract).then_inc(s_w2, 1)

            def scale(t, j):
                pool.wait_ge(s_nrm, t + 1)
                pool.wait_ge(s_out, t + 1)
                nc.gpsimd.tensor_tensor(GM[:], NRM[:], BC[j][:, 1:2].to_broadcast([P, TS, D]),
                                        ALU.mult).then_inc(s_gm, 1)

            def add(t, j):
                pool.wait_ge(s_out, 1 + t + 1)
                pool.wait_ge(s_add, 16 + 16 * TS * t)
                pool.sem_inc(s_clear, 1)
                for k in range(TS):
                    nc.gpsimd.indirect_dma_start(out, bass.IndirectOffsetOnAxis(IDX[j][:, k:k + 1], 0),
                                                 OUT[j][:, k], None, compute_op=ALU.add).then_inc(s_add, 16)

            def tile(t, j, k, last=False):
                bias(t, j, k)
                if not last:
                    low(t + 1, 1 - j)
                scale(t, j)
                add(t, j)

            low(0, 0)
            with pool.Fori(0, HALF) as k:
                tile(2 * k, 0, k)
                tile(2 * k + 1, 1, k)
            tile(NTILE - 1, 0, HALF, last=True)
            pool.wait_ge(s_add, 16 + 16 * TS * NTILE)

        @block.scalar
        def _(act):
            act.sem_inc(s_ge, 4)

            def high(t, j, w, q):
                src, dst, loaded = ((W1s, W1, s_w1s), (W2s, W2, s_w2s))[w]
                cols = slice(q * WC, (q + 1) * WC)
                if q == 0:
                    act.wait_ge(loaded, 16 * (t + 1))
                nc.scalar.copy(dst[j][:, 0, cols], src[:, cols]).then_inc(s_wh, 1)

            def x_high(t, j, c):
                act.wait_ge(s_xp, C * t + c + 1)
                nc.scalar.copy(xT[j][:, 0, c], XP[:, 0:TT]).then_inc(s_xh, 1)

            def prepare(t, j):
                x_high(t, j, 0)
                for q in range(4):
                    high(t, j, 0, q)
                x_high(t, j, 1)
                for q in range(4):
                    high(t, j, 1, q)

            def tile(t, j, k, last=False):
                act.wait_ge(s_x[j], 32 * (k + 1))
                for m in range(FM):
                    act.wait_ge(s_m1, FM * t + m + 1)
                    nc.scalar.activation(hT[:, 0, m], H1[:, m % 4, 0:TT], ACT.Gelu,
                                         bias=B1[j][:, m:m + 1]).then_inc(s_apart, 1)
                    act.wait_ge(s_hl, FM * t + m + 1)
                    nc.scalar.activation(h32[:, m % HRING], H1[:, m % 4, 0:TT], ACT.Gelu,
                                         bias=B1[j][:, m:m + 1]).then_inc(s_ge, 1)
                if not last:
                    prepare(t + 1, 1 - j)

            prepare(0, 0)
            with act.Fori(0, HALF) as k:
                tile(2 * k, 0, k)
                tile(2 * k + 1, 1, k)
            tile(NTILE - 1, 0, HALF, last=True)

        @block.tensor
        def _(pe):
            pe.wait_ge(s_const, 7)

            def turn(t, j, k, c):
                if c == 0:
                    pe.wait_ge(s_x[j], 32 * (k + 1))
                pe.wait_ge(s_xT, 1 + C * t + c)
                for i in range(TS):
                    mm = nc.tensor.transpose(XP[:, P * i:P * i + P], XR[j][:, i, P * c:P * c + P], ident[:])
                mm.then_inc(s_xp, 1)

            def tile(t, j, k, kn):
                pe.wait_ge(s_w1, 8 * (t + 1))
                pe.wait_ge(s_xT, 1 + C * t + C)
                for m in range(FM):
                    pe.wait_ge(s_ge, FM * t + m + 1)
                    for c in range(C):
                        w = [W1[j][:, part, c * F + P * m:c * F + P * m + P] for part in range(2)]
                        for n, (a_, b_) in enumerate(((0, 0), (0, 1), (1, 0))):
                            mm = nc.tensor.matmul(H1[:, m % 4, 0:TT], w[a_], xT[j][:, b_, c],
                                                  start=(c == 0 and n == 0), stop=(c == C - 1 and n == 2))
                    mm.then_inc(s_m1, 1)
                if kn is not None:
                    turn(t + 1, 1 - j, kn, 0)
                pe.wait_ge(s_res, 1 + t)
                pe.wait_ge(s_w2, 4 * (t + 1))
                for m in range(FM):
                    pe.wait_ge(s_hl, HRING + FM * t + m + 1)
                    for i in range(TS):
                        h = [hT[:, part, m, P * i:P * i + P] for part in range(2)]
                        for n, (a_, b_) in enumerate(((0, 0), (0, 1), (1, 0))):
                            mm = nc.tensor.matmul(Y2[:, i, 0:D], h[a_], W2[j][:, b_, D * m:D * m + D],
                                                  start=(m == 0 and n == 0), stop=(m == FM - 1 and n == 2))
                    if m == 3 and kn is not None:
                        turn(t + 1, 1 - j, kn, 1)
                mm.then_inc(s_m2, 1)

            turn(0, 0, 0, 0)
            turn(0, 0, 0, 1)
            with pe.Fori(0, HALF) as k:
                tile(2 * k, 0, k, k)
                tile(2 * k + 1, 1, k, k + 1)
            tile(NTILE - 1, 0, HALF, None)

        @block.vector
        def _(dve):
            v = nc.vector
            count = [0]
            base = [0]
            chain = [s_list]

            def link(ins):
                count[0] += 1
                ins.then_inc(chain[0], 1)
                dve.wait_ge(chain[0], base[0] + count[0])

            def wide(ap):
                return ap[:].rearrange("p (o e) -> p o e", o=1).to_broadcast([P, NTILE, NE])

            dve.wait_ge(s_const, 7)
            link(v.tensor_tensor(cmp[:], run[:].rearrange("p (e o) -> p e o", o=1).to_broadcast([P, NE, MAXT]),
                                 thr[:], ALU.is_gt))
            link(v.tensor_reduce(nt[:], cmp[:], AX.X, ALU.add))
            link(v.tensor_copy(ci[:], nt[:]))
            for e in range(1, NE):
                link(v.tensor_tensor(ci[:, e:e + 1], ci[:, e:e + 1], ci[:, e - 1:e], ALU.add))
            link(v.tensor_tensor(ce[:], ci[:], nt[:], ALU.subtract))
            link(v.tensor_tensor(a[:], tid[:], wide(ci), ALU.is_ge))
            link(v.tensor_reduce(EF[:], a[:], AX.X, ALU.add))
            link(v.tensor_scalar(EF[:], EF[:], float(NE - 1), None, ALU.min))
            link(v.tensor_tensor(z[:], tid[:], wide(ce), ALU.is_ge))
            link(v.tensor_tensor(a[:], z[:], a[:], ALU.subtract))
            link(v.tensor_tensor(z[:], tid[:], wide(ce), ALU.subtract))
            link(v.scalar_tensor_tensor(out=z[:], in0=z[:], scalar=float(TT), in1=eid[:],
                                        op0=ALU.mult, op1=ALU.add))
            link(v.tensor_scalar(z[:], z[:], float(SPARE), None, ALU.subtract))
            link(v.tensor_tensor(z[:], z[:], a[:], ALU.mult))
            link(v.tensor_reduce(SF[:], z[:], AX.X, ALU.add))
            link(v.tensor_scalar(SF[:], SF[:], float(SPARE), None, ALU.add))
            link(v.tensor_copy(SI[:], SF[:]))
            link(v.tensor_copy(EI[:], EF[:]))
            link(v.tensor_tensor(zf[:], run[:], eid[:, 0], ALU.add))
            link(v.tensor_copy(ZI[:], zf[:]))
            assert count[0] <= LIST, count[0]
            dve.sem_inc(s_list, LIST - count[0])
            chain[0] = s_ch

            dve.sem_inc(s_xT, 1)
            dve.sem_inc(s_hl, HRING)
            dve.sem_inc(s_res, 1)
            dve.sem_inc(s_out, 1)

            def turned(t, j, c):
                dve.wait_ge(s_xh, C * t + c + 1)
                v.tensor_tensor(xT[j][:, 1, c], XP[:, 0:TT], xT[j][:, 0, c].bitcast(F32),
                                ALU.subtract).then_inc(s_xT, 1)

            def low(t, j, q):
                cols = slice(q * WC // 2, (q + 1) * WC // 2)
                dve.wait_ge(s_wh, 8 * t + q // 2 + 1)
                v.tensor_tensor(W1[j][:, 1, cols], W1s[:, cols], W1[j][:, 0, cols].bitcast(F32),
                                ALU.subtract).then_inc(s_w1, 1)

            def hidden_low(t, m):
                dve.wait_ge(s_ge, 4 + FM * t + m + 1)
                v.tensor_tensor(hT[:, 1, m], h32[:, m % HRING], hT[:, 0, m].bitcast(F32),
                                ALU.subtract).then_inc(s_hl, 1)

            def several(ops):
                for ins in ops[:-1]:
                    ins.then_inc(s_ch, 1)
                    count[0] += 1
                link(ops[-1])

            def tile(t, j, k, last=False):
                base[0] = t * ECHAIN
                count[0] = 0
                for m in range(FM):
                    hidden_low(t, m)
                    if not last:
                        if m == 3:
                            turned(t + 1, 1 - j, 0)
                        if m >= 4:
                            low(t + 1, 1 - j, 2 * (m - 4))
                            low(t + 1, 1 - j, 2 * (m - 4) + 1)
                if not last:
                    turned(t + 1, 1 - j, 1)
                dve.wait_ge(s_out, 1 + t)
                link(v.tensor_scalar(g[:], XR[j][:, :, E1], EF[:, bass.ds(t, 1)], None, ALU.is_equal))
                link(v.tensor_tensor(g[:], g[:], XR[j][:, :, DG], ALU.mult))
                link(v.tensor_tensor(g[:], g[:], XR[j][:, :, G2], ALU.add))
                dve.wait_ge(s_clear, 1 + t)
                link(v.tensor_copy(IDX[j][:], XR[j][:, :, TOK]))
                dve.wait_ge(s_xb, t + 1)
                dve.wait_ge(s_m2, t + 1)
                v.tensor_tensor(RES[:], Y2[:, :, 0:D], XB[:], ALU.add).then_inc(s_res, 1)
                dve.wait_ge(s_res, 1 + t + 1)
                several([v.bn_stats(st[:, i], RES[:, i]) for i in range(TS)])
                apart(dve)
                several([v.bn_aggr(mv[:, i], st[:, i]) for i in range(TS)])
                rsqrt_steps(v, link, mv[:, :, 1], rs, vh, tt_, LN2_EPS)
                link(v.tensor_tensor(rg[:], rs[:], g[:], ALU.mult))
                dve.wait_ge(s_gm, 1 + t)
                ops = [v.tensor_scalar(NRM[:, i], RES[:, i], mv[:, i, 0:1], rg[:, i:i + 1],
                                       ALU.subtract, ALU.mult) for i in range(TS)]
                ops[-1].then_inc(s_nrm, 1)
                for ins in ops[:-1]:
                    ins.then_inc(s_ch, 1)
                dve.wait_ge(s_gm, 1 + t + 1)
                ops = [v.scalar_tensor_tensor(out=OUT[j][:, i], in0=BC[j][:, 2], scalar=g[:, i:i + 1],
                                              in1=GM[:, i], op0=ALU.mult, op1=ALU.add) for i in range(TS)]
                ops[-1].then_inc(s_out, 1)
                for ins in ops[:-1]:
                    ins.then_inc(s_ch, 1)
                count[0] += 2 * (TS - 1)
                assert count[0] == ECHAIN, count[0]

            turned(0, 0, 0)
            for q in range(8):
                low(0, 0, q)
            turned(0, 0, 1)
            with dve.Fori(0, HALF) as k:
                tile(2 * k, 0, k)
                tile(2 * k + 1, 1, k)
            tile(NTILE - 1, 0, HALF, last=True)


def build(nc, io, xs, out):
    with ExitStack() as ctx:
        keep = {"run": ctx.enter_context(nc.sbuf_tensor("run", [P, NE], F32))}
        attention(nc, io, xs, out, keep)
        experts(nc, io, xs, out, keep)


def kernel(x, cls_tok, L0_tok_W1, L0_tok_b1, L0_tok_W2, L0_tok_b2, L0_attn_Wq, L0_attn_Wk, L0_attn_Wv,
           L0_attn_Wo, L0_ffn_router_w, L0_ffn_w1, L0_ffn_b1, L0_ffn_w2, L0_ffn_b2, L0_ffn_gamma,
           L0_ffn_beta):
    import numpy as np
    import concourse.bacc as bacc
    from concourse.bass_utils import run_bass_kernel_spmd

    def by_pair(w):
        return np.asarray(w).reshape(PAIRS, P, C, P).transpose(0, 3, 2, 1)

    wqkv = np.stack([by_pair(w) for w in (L0_attn_Wq, L0_attn_Wk, L0_attn_Wv)], axis=2)
    arrays = {
        "x": np.asarray(x).reshape(B, X, D),
        "cls": np.asarray(cls_tok).reshape(1, D),
        "wqkv": np.concatenate([wqkv, wqkv[:2]]),
        "wot": np.asarray(L0_attn_Wo).T.reshape(PAIRS, P, D).transpose(1, 0, 2),
        "router": np.asarray(L0_ffn_router_w).reshape(C, P, NE).transpose(1, 0, 2),
        "w1": np.asarray(L0_ffn_w1),
        "b1": np.asarray(L0_ffn_b1).reshape(NE, FM, P).transpose(0, 2, 1),
        "w2": np.asarray(L0_ffn_w2),
        "bc": np.stack([np.asarray(a) for a in (L0_ffn_b2, L0_ffn_gamma, L0_ffn_beta)], axis=1),
    }
    arrays = {k: np.ascontiguousarray(a) for k, a in arrays.items()}
    nc = bacc.Bacc("TRN2", target_bir_lowering=False, num_devices=1)
    io = {k: nc.dram_tensor(f"in_{k}", list(a.shape), F32, kind="ExternalInput").ap() for k, a in arrays.items()}
    xs = nc.dram_tensor("rows", [ROWS, ROW], F32, kind="Internal").ap()
    out = nc.dram_tensor("out", [B * T + TT, D], F32, kind="ExternalOutput").ap()
    build(nc, io, xs, out)
    r = run_bass_kernel_spmd(nc, [{f"in_{k}": a for k, a in arrays.items()}], core_ids=[0])
    return r.results[0]["out"][0:B * T].reshape(B, T, D)
```

```python
from contextlib import ExitStack

import numpy as np
import concourse.bass as bass
from concourse import mybir

F32 = mybir.dt.float32
F32R = mybir.dt.float32r
I32 = mybir.dt.int32
U32 = mybir.dt.uint32
ALU = mybir.AluOpType
ACT = mybir.ActivationFunctionType
AX = mybir.AxisListType

P = 128
B = 4
X = 1024
T = X + 1
D = 256
C = D // P
DH = 64
PAIRS = 8
KT = 9
TP = KT * P
TQ = T + 3
QC = 344
QW = [QC, QC, TQ - 2 * QC]
TAIL = TQ - (T - 1)
NE = 8
F = 1024
FM = F // P
CLAMP = 50.0
SCALE = DH ** -0.5
LN1_EPS = 1e-5
LN2_EPS = 1e-6

TT = 384
TS = TT // P
MAXT = -(-B * T // TT)
NTILE = (2 * B * T + NE * (TT - 1)) // TT
REGION = MAXT * TT + TT
SPARE = NE * REGION
TRASH = SPARE + TT
ROWS = TRASH + 2 * P
ROW, TOK, G2, DG, E1 = D + 4, D, D + 1, D + 2, D + 3



def make_slots():
    s = [dict(n=QC, halves=[(0, 0, 0), (0, 0, QC)]),
         dict(n=QC, halves=[(1, 0, 0), (1, 0, QC)]),
         dict(n=QW[2], halves=[(0, 0, 2 * QC), (1, 0, 2 * QC)])]
    for i in range(1, KT - 1):
        w = TQ - P * i
        if w > 512:
            for h in range(2):
                s.append(dict(n=w // 2, halves=[(h, i, P * i), (h, i, P * i + w // 2)]))
        elif i < KT - 2:
            s.append(dict(n=w, halves=[(0, i, P * i), (1, i, P * i)]))
        else:
            s.append(dict(n=w + TAIL, halves=[(0, i, P * i), (1, i, P * i)], tail=TAIL))
    return s


SLOTS = make_slots()
NS = len(SLOTS)
PMAX = max(2 * s["n"] for s in SLOTS)
THRING = 2
PRING = 7
assert (2 * NS) % PRING == 0 and NS % 2 == 0
UNITS = [[n for n, s in enumerate(SLOTS) if s["halves"][0][1] == i] for i in range(KT - 1)]
NU = len(UNITS)
UNIT_OF = {n: u for u, ns in enumerate(UNITS) for n in ns}
DIAG = [n for n in range(NS) if n != 2]
CHUNK_UNIT = [2, 5, 7]
CHUNK_SLOT = [max(UNITS[u]) for u in CHUNK_UNIT]


def masks_through(n):
    return sum(1 for m in DIAG if m <= n)


DSUMS = 9


def pool_sums_through(n):
    return n + 1 - DSUMS + (n == NS - 1)


PSUMS = pool_sums_through(NS - 1)
HRING = 4
ECHAIN = 28
CHAIN = 135


def pv_pieces(u):
    by_head = [[], []]
    for n in UNITS[u]:
        s = SLOTS[n]
        tail = s.get("tail", 0)
        for k, (h, i, q0) in enumerate(s["halves"]):
            runs = [(i, q0, q0 + s["n"] - tail, k * s["n"])]
            if tail:
                runs.append((i + 1, T - 1, TQ, (k + 1) * s["n"] - tail))
            for i_, a, b, col in runs:
                while a < b:
                    c = a // QC
                    e = min(b, (c + 1) * QC)
                    by_head[h].append((n, col, h, i_, c, a, e))
                    col += e - a
                    a = e
    return [p for pair in zip(*by_head) for p in pair]


UNIT_AT = {0: (5, -1), 1: (6, -1), 2: (7, -1), 7: (0, 0), 8: (1, 0), 10: (2, 0), 12: (3, 0), 13: (4, 0)}
SUM_LAG = 3
RECIP_AT = {0: (1, 0), 1: (1, 1), 2: (2, 0), 3: (2, 1), 12: (0, 0), 13: (0, 1)}
DEN1, DEN2, DEN0 = ("den", 1), ("den", 2), ("den", 0)
PLAIN = [[DEN1], [("q", 0)], [DEN2], [("q", 1)], [("q", 2)], [("k", 0)], [("k", 1)], [("k", 2)],
         [("v", 0)], [("v", 1)], [], [("v", 2)], [DEN0], []]
PROJ = [(k, c) for k in "qkv" for c in range(3)]
TURN = 5


def with_jobs(extra):
    return [jobs + ([extra[n]] if n in extra else []) for n, jobs in enumerate(PLAIN)]


JOBS = {
    "plain": PLAIN,
    "first": [[j for j in jobs if j not in (DEN1, DEN2)] for jobs in PLAIN],
    "last": [[j for j in jobs if j[0] == "den"] for jobs in PLAIN],
    "norm": PLAIN,
    "turn": [[DEN1, ("x", 0)], [("x", 1), ("x", 2)], [DEN2, ("x", 3)], [("x", 4)], [("q", 0)], [("q", 1)],
             [("q", 2)], [("k", 0)], [("k", 1)], [("k", 2)], [("v", 0)], [("v", 1)], [DEN0, ("v", 2)], []],
    "out": with_jobs({2: ("o", 0), 3: ("o", 1), 5: ("o", 2), 6: ("o", 3), 7: ("o", 4), 8: ("o", 5),
                      9: ("o", 6), 10: ("o", 7), 11: ("o", 8)}),
    "norm2": with_jobs({9: ("y", 0), 10: ("y", 1), 11: ("y", 2), 12: ("y", 3), 13: ("y", 4)}),
    "route": with_jobs({0: ("r", 0), 9: ("n", 0)}),
    "place": PLAIN,
}
LEAD = 4
KINDS = ["first"] + ["plain"] * 5 + ["norm", "turn", "out", "norm2", "route", "place"]
LAST_KINDS = ["plain"] * 3 + ["last"]
FULL = [("q", 0), ("r", 0), ("n", 0)]
NO_PAIR = [("o", t) for t in range(KT)] + [("y", k) for k in range(TURN)] + [("r", 0), ("n", 0)]


def job_count(kind):
    return sum(len(jobs) for jobs in JOBS[kind])


def jobs_before(i, q):
    lead = TURN + len(PROJ) + sum(job_count(k) for k in KINDS[:min(q, LEAD)])
    if q < LEAD:
        return lead
    return lead + i * sum(job_count(k) for k in KINDS[LEAD:]) + sum(job_count(k) for k in KINDS[LEAD:q])


def index_of(kind, job):
    return [j for jobs in JOBS[kind] for j in jobs].index(job)


def turn_views(k):
    if k < TURN - 1:
        return [(k // 2, 4 * (k % 2) + t) for t in range(4)]
    return [(c, KT - 1) for c in range(C)]


def attention(nc, io, xs, out, keep):
    x, cls, wqkv, wot, router = io["x"], io["cls"], io["wqkv"], io["wot"], io["router"]
    with ExitStack() as ctx:
        def sb(name, shape, dt=F32):
            return ctx.enter_context(nc.sbuf_tensor(name, shape, dt))

        def sem(name):
            return ctx.enter_context(nc.semaphore(name))

        H = sb("H", [P, KT, D])
        XN = sb("XN", [P, KT, ROW])
        xnT = sb("xnT", [P, C, TP])
        W = [sb(f"W{j}", [P, 3, C, P]) for j in range(2)]
        WO = sb("WO", [P, PAIRS, D])
        R = sb("R", [P, C, NE])
        raw = sb("raw", [P, 2, QC])
        qN = sb("qN", [P, 2, TQ], F32R)
        kN = sb("kN", [P, 2, TQ], F32R)
        q4 = [sb(f"q4_{j}", [P, 2, 2, TQ], F32R) for j in range(2)]
        kS = [sb(f"kS_{j}", [P, 2, TP], F32R) for j in range(2)]
        V = [sb(f"V_{j}", [P, KT, P]) for j in range(2)]
        TH = sb("TH", [P, THRING, PMAX])
        PR = sb("PR", [P, PRING, PMAX])
        SUM = sb("SUM", [P, 2, TQ])
        RC = sb("RC", [P, 3, QC])
        OT = sb("OT", [P, PAIRS, TQ])
        ones = sb("ones", [P, P])
        upper = sb("upper", [P, P])
        st = sb("st", [P, KT, 6])
        mv = sb("mv", [P, KT, 2])
        rs = sb("rs", [P, KT])
        vh = sb("vh", [P, KT])
        nt = sb("nt", [P, KT])
        lg = sb("lg", [P, KT, NE])
        top = sb("top", [P, KT, NE])
        ti = sb("ti", [P, KT, NE], U32)
        tf = sb("tf", [P, KT, 2])
        M = sb("M", [P, 2, KT, NE])
        CC = sb("CC", [P, KT, NE])
        rank = sb("rank", [P, KT, NE])
        mr = sb("mr", [P, 2, KT, NE])
        pf = sb("pf", [P, 2, KT])
        pi = sb("pi", [P, 2, KT], I32)
        eg = sb("eg", [P, 2, KT])
        gate = sb("gate", [P, KT])
        iota_e = sb("iota_e", [P, KT, NE])
        valid = sb("valid", [P, KT, NE])
        trash = sb("trash", [P, 2, KT])
        tok = sb("tok", [P, KT])
        rk = sb("rk", [P, 200])
        run, ident, EF, EI, SI = (keep[k] for k in ("run", "ident", "EF", "EI", "SI"))
        ZI = sb("ZI", [P, NE], I32)
        room, taken = PR[:].rearrange("p r q -> p (r q)"), [0]

        def view(*shape):
            n = int(np.prod(shape))
            v = room[:, taken[0]:taken[0] + n]
            taken[0] += n
            if len(shape) == 2:
                v = v.rearrange("p (a b) -> p a b", a=shape[0])
            return v

        fill = view(TS, ROW)
        thr, cmp = view(NE, MAXT), view(NE, MAXT)
        ntiles, ce, ci, zf = (view(NE) for _ in range(4))
        tid, eid, a, z = (view(NTILE, NE) for _ in range(4))
        SF = view(NTILE)
        yT = OT[:, 5:8].rearrange("p a q -> p (a q)")[:, 0:C * TP].rearrange("p (c q) -> p c q", c=C)

        S = ctx.enter_context(nc.psum_tensor("S", [P, 4, 512], F32))
        O = ctx.enter_context(nc.psum_tensor("O", [P, 3, 512], F32))
        AUX = ctx.enter_context(nc.psum_tensor("AUX", [P, 512], F32))

        s_const = sem("s_const")
        s_zero = sem("s_zero")
        s_wo = sem("s_wo")
        s_w = [sem("s_w0"), sem("s_w1")]
        s_h = sem("s_h")
        s_x = sem("s_x")
        s_dve = sem("s_dve")
        s_xn = sem("s_xn")
        s_yn = sem("s_yn")
        s_aux = sem("s_aux")
        s_hi = sem("s_hi")
        s_lo = sem("s_lo")
        s_evac = sem("s_evac")
        s_qd = sem("s_qd")
        s_kd = sem("s_kd")
        s_qk = sem("s_qk")
        s_th = sem("s_th")
        s_ex = sem("s_ex")
        s_mask = sem("s_mask")
        s_sum = sem("s_sum")
        s_psum = sem("s_psum")
        s_pv = sem("s_pv")
        s_rc = sem("s_rc")
        s_norm = sem("s_norm")
        s_ge = sem("s_ge")
        s_cc = sem("s_cc")
        s_pos = sem("s_pos")
        s_sc = sem("s_sc")
        s_hs = sem("s_hs")
        s_placed = sem("s_placed")
        s_listed = sem("s_listed")
        s_fill = sem("s_fill")
        s_apart = sem("s_apart")

        def apart(eng):
            eng.sem_inc(s_apart, 1)

        def add_to_sums(ops, eng, j, n, signal, first_done):
            s = SLOTS[n]
            (h0, _, q0), (h1, _, _) = s["halves"]
            w, tail = s["n"], s.get("tail", 0)
            pr = PR[:, (j * NS + n) % PRING, 0:2 * w]
            if h0 == h1:
                dst, src = SUM[:, h0, q0:q0 + 2 * w], pr
            else:
                pr = pr.rearrange("p (h q) -> p h q", h=2)
                dst, src = SUM[:, :, q0:q0 + w - tail], pr[:, :, 0:w - tail]
            ops.tensor_tensor(dst, dst, src, ALU.add).then_inc(signal, 1)
            if tail:
                eng.wait_ge(signal, first_done)
                dst = SUM[0:1, :, T - 1:TQ]
                ops.tensor_tensor(dst, dst, pr[0:1, :, w - tail:w], ALU.add).then_inc(signal, 1)

        last_jobs = jobs_before(B - 1, PAIRS - 1) + job_count("last")

        def last_round(i):
            return isinstance(i, int) and i == B - 1

        def rounds(engine, pair, tail):
            for q in range(LEAD):
                pair(0, q, KINDS[q], q)
            with engine.Fori(0, B - 1) as i:
                for q in range(LEAD, LEAD + PAIRS):
                    pair(i, q, KINDS[q], q % PAIRS)
            for q in range(LEAD, PAIRS):
                pair(B - 1, q, LAST_KINDS[q - LEAD], q)
            tail()

        block = ctx.enter_context(nc.Block())

        @block.sync
        def _(sp):
            def load(dst, b, signal):
                sp.dma_start(dst[0:1, 0, 0:D], cls).then_inc(signal, 16)
                sp.dma_start(dst[1:P, 0, 0:D], x[b, 0:P - 1]).then_inc(signal, 16)
                sp.dma_start(dst[:, 1:KT - 1, 0:D],
                             x[b, P - 1:X - 1].rearrange("(t p) d -> p t d", p=P)).then_inc(signal, 16)
                sp.dma_start(dst[0:1, KT - 1, 0:D], x[b, X - 1:X]).then_inc(signal, 16)

            def spread(j, g):
                def half(dst, src, s):
                    sp.dma_start(dst.bitcast(F32), src.bitcast(F32)).then_inc(s, 16)

                sp.wait_ge(s_lo, 2 + 6 * g + 3)
                for h in range(2):
                    for o in range(2):
                        half(q4[j][64 * o:64 * o + 64, h], qN[64 * h:64 * h + 64], s_qd)
                sp.wait_ge(s_lo, 2 + 6 * g + 6)
                for h in range(2):
                    for part in range(2):
                        half(kS[j][64 * part:64 * part + 64, h, 0:TQ],
                             kN[64 * h:64 * h + 64, part], s_kd)

            def store(i, done):
                sp.wait_ge(s_evac, 1 + done)
                apart(sp)
                sp.dma_start(out[bass.ds(i * T, X)].rearrange("(t p) d -> p t d", p=P),
                             H[:, 0:KT - 1]).then_inc(s_hs, 16)
                sp.dma_start(out[bass.ds(i * T + X, 1)], H[0:1, KT - 1]).then_inc(s_hs, 16)

            def pair(i, q, kind, p):
                g = i * PAIRS + q
                if kind == "norm2":
                    store(i, jobs_before(i, q))
                if p == LEAD:
                    sp.wait_ge(s_placed, i + 1)
                    apart(sp)
                    if not last_round(i):
                        load(XN, i + 1, s_x)
                    load(H, i, s_h)
                j = q % 2
                if not (last_round(i) and p + 2 >= PAIRS):
                    sp.wait_ge(s_aux, jobs_before(i, q))
                    apart(sp)
                    sp.dma_start(W[j][:], wqkv[(p + 2) % PAIRS]).then_inc(s_w[j], 16)
                if kind != "last":
                    spread(1 - j, g + 1)

            def tail():
                store(B - 1, last_jobs + 2 + KT)

            sp.wait_ge(s_zero, 1)
            load(XN, 0, s_x)
            for j in range(2):
                sp.dma_start(W[j][:], wqkv[j]).then_inc(s_w[j], 16)
            sp.dma_start(WO[:], wot).then_inc(s_wo, 16)
            sp.dma_start(R[:], router).then_inc(s_wo, 16)
            spread(0, 0)
            rounds(sp, pair, tail)
            sp.wait_ge(s_const, 15)
            sp.dma_start(xs[SPARE:SPARE + TT].rearrange("(t p) d -> p t d", p=P), fill).then_inc(s_fill, 16)
            sp.wait_ge(s_listed, 1)
            with sp.Fori(0, NE) as e:
                row = sp.value_load(ZI[0:1, bass.ds(e, 1)], min_val=0, max_val=SPARE - TT)
                sp.dma_start(xs[bass.ds(row, TT)].rearrange("(t p) d -> p t d", p=P), fill).then_inc(s_fill, 16)
            sp.wait_ge(s_fill, 16 * (1 + NE))
            sp.wait_ge(s_hs, B * 32)

        @block.gpsimd
        def _(pool):
            nc.gpsimd.memset(ones[:], 1.0).then_inc(s_const, 1)
            pool.wait_ge(s_const, 1)
            nc.gpsimd.affine_select(out=ident[:], in_=ones[:], compare_op=ALU.is_equal, fill=0.0,
                                    base=0, pattern=[[-1, P]], channel_multiplier=1).then_inc(s_const, 1)
            nc.gpsimd.affine_select(out=upper[:], in_=ones[:], compare_op=ALU.is_gt, fill=0.0,
                                    base=0, pattern=[[1, P]], channel_multiplier=-1).then_inc(s_const, 1)
            nc.gpsimd.iota(iota_e[:], pattern=[[0, KT], [1, NE]], base=0, channel_multiplier=0,
                           allow_small_or_imprecise_dtypes=True).then_inc(s_const, 1)
            nc.gpsimd.memset(valid[:], 1.0).then_inc(s_const, 1)
            pool.wait_ge(s_const, 5)
            nc.gpsimd.affine_select(out=valid[:, KT - 1], in_=valid[:, KT - 1], compare_op=ALU.is_ge,
                                    fill=0.0, base=0, pattern=[[0, NE]],
                                    channel_multiplier=-1).then_inc(s_const, 1)
            nc.gpsimd.iota(trash[:], pattern=[[P, 2], [0, KT]], base=TRASH, channel_multiplier=1,
                           allow_small_or_imprecise_dtypes=True).then_inc(s_const, 1)
            pool.wait_ge(s_const, 7)
            nc.gpsimd.memset(trash[:, :, 0:KT - 1], 0.0).then_inc(s_const, 1)
            nc.gpsimd.memset(trash[0:1, :, KT - 1:KT], 0.0).then_inc(s_const, 1)
            nc.gpsimd.iota(tok[:], pattern=[[P, KT]], base=0, channel_multiplier=1,
                           allow_small_or_imprecise_dtypes=True).then_inc(s_const, 1)

            pool.sem_inc(s_lo, 2)
            pool.sem_inc(s_psum, PSUMS)

            def mask(g, j, n):
                if n not in DIAG:
                    return
                s = SLOTS[n]
                h0, h1 = s["halves"]
                pool.wait_ge(s_ex, 2 + g * NS + n + 1)
                apart(pool)
                pr = PR[:, (j * NS + n) % PRING, 0:2 * s["n"]]
                if h0[0] == h1[0]:
                    v, pat = pr[:, 0:P], [[1, P]]
                else:
                    v = pr.rearrange("p (h q) -> p h q", h=2)[:, :, 0:P]
                    pat = [[0, 2], [1, P]]
                nc.gpsimd.affine_select(out=v, in_=v, compare_op=ALU.is_ge, fill=0.0, base=0,
                                        pattern=pat, channel_multiplier=-1).then_inc(s_mask, 1)

            def sums(g, j, n):
                if n < DSUMS:
                    return
                if n == DSUMS:
                    pool.wait_ge(s_sum, DSUMS + (g + 1) * DSUMS)
                pool.wait_ge(s_mask, g * len(DIAG) + masks_through(n))
                if n > DSUMS:
                    pool.wait_ge(s_psum, PSUMS + g * PSUMS + pool_sums_through(n - 1))
                add_to_sums(nc.gpsimd, pool, j, n, s_psum, PSUMS + g * PSUMS + pool_sums_through(n - 1) + 1)

            def low(g, what, c):
                i = 3 * "qk".index(what) + c
                dst = (qN, kN)["qk".index(what)]
                cols = slice(c * QC, c * QC + QW[c])
                pool.wait_ge(s_hi, 6 * g + i + 1)
                nc.gpsimd.tensor_tensor(dst[:, 1, cols], raw[:, i % 2, 0:QW[c]], dst[:, 0, cols].bitcast(F32),
                                        ALU.subtract).then_inc(s_lo, 1)

            def slot(g, j, n):
                mask(g, j, n)
                sums(g, j, n)

            def place(i, t):
                for k in range(2):
                    nc.gpsimd.indirect_dma_start(xs, bass.IndirectOffsetOnAxis(pi[:, k, t:t + 1], 0),
                                                 XN[:, t], None).then_inc(s_sc, 16)

            def pair(i, q, kind, p):
                g = i * PAIRS + q
                if kind == "place":
                    pool.wait_ge(s_pos, i + 1)
                    apart(pool)
                for n in range(NS):
                    if n >= 1:
                        slot(g, q % 2, n - 1)
                    elif kind != "first":
                        slot(g - 1, 1 - q % 2, NS - 1)
                    if n >= 1:
                        for what, c in JOBS[kind][n - 1]:
                            if what in "qk":
                                low(g + 1, what, c)
                    if kind == "place" and 1 <= n < KT + 1:
                        place(i, n - 1)
                if kind == "place":
                    pool.wait_ge(s_sc, (i + 1) * KT * 2 * 16)
                    apart(pool)
                    pool.wait_ge(s_hs, (i + 1) * 32)
                    pool.sem_inc(s_placed, 1)

            def tail():
                slot(B * PAIRS - 1, 1, NS - 1)
                pool.wait_ge(s_psum, PSUMS + B * PAIRS * PSUMS)
                pool.wait_ge(s_sum, DSUMS + B * PAIRS * DSUMS)
                pool.wait_ge(s_pv, NU + B * PAIRS * NU)
                nc.gpsimd.memset(fill, 0.0).then_inc(s_const, 1)
                pool.wait_ge(s_const, 11)
                nc.gpsimd.iota(fill[:, :, TOK], pattern=[[P, TS]], base=B * T, channel_multiplier=1,
                               allow_small_or_imprecise_dtypes=True).then_inc(s_const, 1)
                nc.gpsimd.iota(thr, pattern=[[0, NE], [TT, MAXT]], base=0, channel_multiplier=0,
                               allow_small_or_imprecise_dtypes=True).then_inc(s_const, 1)
                nc.gpsimd.iota(tid, pattern=[[1, NTILE], [0, NE]], base=0, channel_multiplier=0,
                               allow_small_or_imprecise_dtypes=True).then_inc(s_const, 1)
                nc.gpsimd.iota(eid, pattern=[[0, NTILE], [REGION, NE]], base=0, channel_multiplier=0,
                               allow_small_or_imprecise_dtypes=True).then_inc(s_const, 1)
                pool.wait_ge(s_pos, B)
                for t in range(KT):
                    place(B - 1, t)

            pool.sem_inc(s_placed, 1)
            for what, c in PROJ[:6]:
                low(0, what, c)
            rounds(pool, pair, tail)
            pool.wait_ge(s_sc, B * KT * 2 * 16)

        @block.scalar
        def _(act):
            act.sem_inc(s_th, 2)
            act.sem_inc(s_ex, 2)

            def hi(g, what, c, done):
                k = "qk".index(what)
                act.wait_ge(s_evac, 1 + done + 1)
                nc.scalar.copy((qN, kN)[k][:, 0, c * QC:c * QC + QW[c]],
                               raw[:, (3 * k + c) % 2, 0:QW[c]]).then_inc(s_hi, 1)

            def tanh(g, j, n):
                s = SLOTS[n]
                act.wait_ge(s_qk, g * NS + n + 1)
                act.wait_ge(s_ex, 2 + g * NS + n - THRING + 1)
                nc.scalar.activation(
                    TH[:, (j * NS + n) % THRING, 0:2 * s["n"]].rearrange("p (h q) -> p h q", h=2),
                    S[:, 2 * (n % 2):2 * (n % 2) + 2, 0:s["n"]], ACT.Tanh,
                    scale=SCALE / CLAMP).then_inc(s_th, 1)

            def exp(g, j, n):
                s = SLOTS[n]
                act.wait_ge(s_th, 2 + g * NS + n + 1)
                m, ago = (n - PRING, 0) if n >= PRING else (n - PRING + NS, 1)
                act.wait_ge(s_pv, (1 - ago) * NU + g * NU + UNIT_OF[m] + 1)
                if m < DSUMS:
                    act.wait_ge(s_sum, (1 - ago) * DSUMS + g * DSUMS + m + 1)
                else:
                    act.wait_ge(s_psum, (1 - ago) * PSUMS + g * PSUMS + pool_sums_through(m))
                nc.scalar.activation(PR[:, (j * NS + n) % PRING, 0:2 * s["n"]],
                                     TH[:, (j * NS + n) % THRING, 0:2 * s["n"]], ACT.Exp,
                                     scale=CLAMP).then_inc(s_ex, 1)

            def gates(i):
                act.wait_ge(s_ge, 2 * i + 1)
                nc.scalar.activation(eg[:, 0], eg[:, 1], ACT.Exp).then_inc(s_ge, 1)

            def pair(i, q, kind, p):
                g, j = i * PAIRS + q, q % 2
                done = jobs_before(i, q)
                for n in range(NS):
                    if n >= 1:
                        for what, c in JOBS[kind][n - 1]:
                            if what in "qk":
                                hi(g + 1, what, c, done + index_of(kind, (what, c)))
                    tanh(g, j, n)
                    if n >= 1:
                        exp(g, j, n - 1)
                    elif kind != "first":
                        exp(g - 1, 1 - j, NS - 1)
                    if kind == "route" and n == 7:
                        gates(i)

            def tail():
                exp(B * PAIRS - 1, 1, NS - 1)
                gates(B - 1)

            for jj, (what, c) in enumerate(PROJ[:6]):
                hi(0, what, c, TURN + jj)
            rounds(act, pair, tail)

        @block.tensor
        def _(pe):
            def qk(g, j, n):
                s = SLOTS[n]
                if n == 0:
                    pe.wait_ge(s_qd, 64 * (g + 1))
                    pe.wait_ge(s_kd, 64 * (g + 1))
                pe.wait_ge(s_th, g * NS + n + 1)
                tail = s.get("tail", 0)
                for k, (h, i, q0) in enumerate(s["halves"]):
                    out = S[:, 2 * (n % 2) + k]
                    runs = [(i, q0, 0, s["n"] - tail)]
                    if tail:
                        runs.append((i + 1, T - 1, s["n"] - tail, s["n"]))
                    for i_, q, a, e in runs:
                        for part in range(2):
                            mm = nc.tensor.matmul(out[:, a:e], kS[j][:, h, P * i_:P * i_ + P],
                                                  q4[j][:, h, part, q:q + e - a],
                                                  start=(part == 0), stop=(part == 1))
                mm.then_inc(s_qk, 1)

            def pv(g, j, u):
                n = max(UNITS[u])
                if u == 0:
                    pe.wait_ge(s_norm, 3 + 3 * g)
                    pe.wait_ge(s_ex, 2 + g * NS + n + 1)
                pe.wait_ge(s_mask, g * len(DIAG) + masks_through(n))
                for n_, col, h, i, c, a, e in pv_pieces(u):
                    K = 1 if i == KT - 1 else P
                    last = i == CHUNK_LAST[c]
                    mm = nc.tensor.matmul(O[64 * h:64 * h + 64, c, a - c * QC:e - c * QC],
                                          V[j][0:K, i, 64 * h:64 * h + 64],
                                          PR[0:K, (j * NS + n_) % PRING, col:col + e - a],
                                          start=(i == 0), stop=last, skip_group_check=True)
                mm.then_inc(s_pv, 1)

            CHUNK_LAST = [2, 5, KT - 1]

            def job(kind, c, j, g, loads, done, i, bank=None):
                if kind in "xy" and c == 0:
                    pe.wait_ge((s_xn, s_yn)["xy".index(kind)], i + 1)
                if kind == "o":
                    last = min(P * c + P, T) - 1
                    pe.wait_ge(s_norm, 3 + 3 * (g - 1) + last // QC + 1)
                if kind == "n":
                    pe.wait_ge(s_cc, i + 1)
                A = AUX if bank is None else S[:, bank % 4]
                if bank is None or (kind, c) in FULL:
                    pe.wait_ge(s_evac, 1 + done)
                elif bank >= 4:
                    pe.wait_ge(s_evac, 1 + done - 3)
                if kind in "xy":
                    for m, (ci, t) in enumerate(turn_views(c)):
                        mm = nc.tensor.transpose(A[:, P * m:P * m + P], XN[:, t, P * ci:P * ci + P], ident[:])
                elif kind == "o":
                    m = P if c < KT - 1 else 1
                    for p in range(PAIRS):
                        mm = nc.tensor.matmul(A[0:m, 0:D], OT[:, p, P * c:P * c + m], WO[:, p],
                                              start=(p == 0), stop=(p == PAIRS - 1))
                elif kind == "r":
                    for t in range(KT):
                        for ci in range(C):
                            mm = nc.tensor.matmul(A[:, NE * t:NE * t + NE], yT[:, ci, P * t:P * t + P],
                                                  R[:, ci], start=(ci == 0), stop=(ci == C - 1))
                elif kind == "n":
                    chosen = CC[:].rearrange("p t e -> p (t e)")
                    nc.tensor.matmul(A[:, 0:KT * NE], upper[:], chosen, start=True, stop=True)
                    mm = nc.tensor.matmul(A[:, 128:128 + KT * NE], ones[:], chosen, start=True, stop=True)
                elif kind in "qk":
                    w = "qk".index(kind)
                    if kind == "q" and c == 0:
                        pe.wait_ge(s_w[j], 16 * loads)
                    for ci in range(C):
                        mm = nc.tensor.matmul(A[:, 0:QW[c]], W[j][:, w, ci],
                                              xnT[:, ci, c * QC:c * QC + QW[c]],
                                              start=(ci == 0), stop=(ci == C - 1))
                elif kind == "v":
                    for t in range(3):
                        for ci in range(C):
                            tok = P * (3 * c + t)
                            mm = nc.tensor.matmul(A[:, P * t:P * t + P], xnT[:, ci, tok:tok + P],
                                                  W[j][:, 2, ci], start=(ci == 0), stop=(ci == C - 1))
                else:
                    m = CHUNK_SLOT[c]
                    if m < DSUMS:
                        pe.wait_ge(s_sum, DSUMS + g * DSUMS + m + 1)
                    else:
                        pe.wait_ge(s_psum, PSUMS + g * PSUMS + pool_sums_through(m))
                    for h in range(2):
                        mm = nc.tensor.matmul(A[64 * h:64 * h + 64, 0:QW[c]], ones[:, 0:64],
                                              SUM[:, h, c * QC:c * QC + QW[c]],
                                              start=True, stop=True, skip_group_check=True)
                mm.then_inc(s_aux, 1)

            def run_job(i, q, kind, what, c):
                g, j = i * PAIRS + q, q % 2
                done = jobs_before(i, q) + index_of(kind, (what, c))
                if what in "qkv":
                    job(what, c, 1 - j, None, i * (PAIRS // 2) + (q + 1) // 2 + 1, done, None)
                elif what == "den" and c > 0:
                    job(what, c, 1 - j, g - 1, None, done, None)
                elif what == "x":
                    job(what, c, None, None, None, done, i + 1)
                else:
                    job(what, c, j, g, None, done, i)

            def pair(i, q, kind, p):
                g, j = i * PAIRS + q, q % 2
                for n in range(NS):
                    qk(g, j, n)
                    for what, c in JOBS[kind][n][:1]:
                        run_job(i, q, kind, what, c)
                    if n in UNIT_AT:
                        u, off = UNIT_AT[n]
                        if off == 0:
                            pv(g, j, u)
                        elif kind != "first":
                            pv(g - 1, 1 - j, u)
                    for what, c in JOBS[kind][n][1:]:
                        run_job(i, q, kind, what, c)

            def tail():
                g = B * PAIRS - 1
                done = last_jobs
                pv(g, 1, 5)
                job("den", 1, 1, g, None, done, None)
                pv(g, 1, 6)
                pv(g, 1, 7)
                job("den", 2, 1, g, None, done + 1, None)
                pe.wait_ge(s_th, 2 + B * PAIRS * NS)
                for k, (what, c) in enumerate(NO_PAIR):
                    job(what, c, None, g + 1, None, done + 2 + k, B - 1, bank=k)

            pe.sem_inc(s_pv, NU)
            pe.wait_ge(s_const, 10)
            for k in range(TURN):
                job("x", k, None, None, None, k, 0, bank=k)
            for k, (what, c) in enumerate(PROJ):
                job(what, c, 0, None, 1, TURN + k, None, bank=TURN + k)
            pe.wait_ge(s_evac, 1 + TURN + len(PROJ))
            pe.wait_ge(s_wo, 32)
            rounds(pe, pair, tail)

        @block.vector
        def _(dve):
            v = nc.vector
            zeros = [H[:, KT - 1], XN[:, KT - 1], run[:]]
            for j in range(2):
                zeros.append(kS[j][:, :, T:TP].bitcast(F32))
            for pad in zeros:
                v.memset(pad, 0.0).then_inc(s_dve, 1)
            dve.wait_ge(s_dve, len(zeros))
            dve.sem_inc(s_zero, 1)
            dve.sem_inc(s_sum, DSUMS)
            dve.sem_inc(s_evac, 1)
            dve.sem_inc(s_norm, 3)
            dve.wait_ge(s_const, 10)
            count = [len(zeros)]
            base = [0]

            def link(ins):
                count[0] += 1
                ins.then_inc(s_dve, 1)
                dve.wait_ge(s_dve, base[0] + count[0])

            def several(ops):
                for ins in ops[:-1]:
                    ins.then_inc(s_dve, 1)
                    count[0] += 1
                link(ops[-1])

            NORM_PARTS = 9

            def layernorm(src, eps, part):
                tiles = range(3 * (part % 6), 3 * (part % 6) + 3)
                if part < 3:
                    several([v.bn_stats(st[:, t], src[:, t, 0:D]) for t in tiles])
                elif part == 3:
                    apart(dve)
                    several([v.bn_aggr(mv[:, t], st[:, t]) for t in range(KT)])
                elif part == 4:
                    rsqrt_guess(v, link, mv[:, :, 1], rs, vh, nt, eps)
                    rsqrt_newton(v, link, rs, vh, nt, 1)
                elif part == 5:
                    rsqrt_newton(v, link, rs, vh, nt, 2)
                else:
                    several([v.tensor_scalar(XN[:, t, 0:D], src[:, t, 0:D], mv[:, t, 0:1], rs[:, t:t + 1],
                                             ALU.subtract, ALU.mult) for t in tiles])

            def first_norm(b, part):
                if part == 0:
                    dve.wait_ge(s_x, 64 * (b + 1))
                layernorm(XN, LN1_EPS, part)
                if part == NORM_PARTS - 1:
                    dve.sem_inc(s_xn, 1)

            def second_norm_stats(t, done):
                dve.wait_ge(s_evac, 1 + done + 1)
                ins = v.bn_stats(st[:, t], H[:, t])
                if t == KT - 1:
                    link(ins)
                else:
                    ins.then_inc(s_dve, 1)
                    count[0] += 1

            def second_norm(part):
                layernorm(H, LN1_EPS, part)
                if part == NORM_PARTS - 1:
                    dve.sem_inc(s_yn, 1)

            def read_out(what, c, j, g, done, i, bank=None):
                if what == "o" and c == 0:
                    dve.wait_ge(s_h, 64 * (i + 1))
                A = AUX if bank is None else S[:, bank % 4]
                dve.wait_ge(s_aux, done + 1)
                if what in "xy":
                    dst = (xnT[:], yT)["xy".index(what)]
                    if c < TURN - 1:
                        v.tensor_copy(dst[:, c // 2, 512 * (c % 2):512 * (c % 2) + 512], A[:, 0:512]).then_inc(s_evac, 1)
                    else:
                        v.tensor_copy(dst[:, :, X:TP],
                                      A[:, 0:C * P].rearrange("p (c q) -> p c q", c=C)).then_inc(s_evac, 1)
                elif what == "o":
                    m = P if c < KT - 1 else 1
                    v.tensor_tensor(H[0:m, c], H[0:m, c], A[0:m, 0:D], ALU.add).then_inc(s_evac, 1)
                elif what == "r":
                    v.tensor_copy(lg[:].rearrange("p t e -> p (t e)"), A[:, 0:KT * NE]).then_inc(s_evac, 1)
                elif what == "n":
                    v.tensor_copy(rk[:, 0:KT * NE], A[:, 0:KT * NE]).then_inc(s_dve, 1)
                    count[0] += 1
                    v.tensor_copy(rk[:, 128:128 + KT * NE], A[:, 128:128 + KT * NE]).then_inc(s_evac, 1)
                elif what in "qk":
                    i = 3 * "qk".index(what) + c
                    dve.wait_ge(s_lo, 6 * g + i + 1)
                    v.tensor_copy(raw[:, i % 2, 0:QW[c]], A[:, 0:QW[c]]).then_inc(s_evac, 1)
                else:
                    v.tensor_copy(V[j][:, 3 * c:3 * c + 3],
                                  A[:, 0:3 * P].rearrange("p (t f) -> p t f", t=3)).then_inc(s_evac, 1)

            def sums(g, j, n, done):
                if n in DIAG:
                    dve.wait_ge(s_mask, g * len(DIAG) + masks_through(n))
                else:
                    dve.wait_ge(s_ex, 2 + g * NS + n + 1)
                (h0, i, q0), (h1, _, q1) = SLOTS[n]["halves"]
                w = SLOTS[n]["n"]
                if i == 0:
                    dve.wait_ge(s_aux, done)
                    pr = PR[:, (j * NS + n) % PRING, 0:2 * w]
                    if h0 == h1:
                        dst = SUM[:, h0, q0:q0 + 2 * w]
                    else:
                        pr, dst = pr.rearrange("p (h q) -> p h q", h=2), SUM[:, :, q0:q0 + w]
                    v.tensor_copy(dst, pr).then_inc(s_sum, 1)
                else:
                    dve.wait_ge(s_sum, DSUMS + g * DSUMS + max(n - 1, 3))
                    add_to_sums(v, dve, j, n, s_sum, None)

            def take_den(g, c, done):
                dve.wait_ge(s_aux, done + 1)
                dve.wait_ge(s_norm, 3 * g + c + 1)
                v.tensor_copy(RC[:, c, 0:QW[c]], AUX[:, 0:QW[c]]).then_inc(s_evac, 1)

            def normalise(g, p, c, half, done):
                w = QW[c] // 2
                part = RC[:, c, half * w:half * w + w]
                dve.wait_ge(s_evac, 1 + done + 1)
                v.reciprocal(part, part).then_inc(s_rc, 1)
                if half == 0:
                    return
                dve.wait_ge(s_rc, 6 * g + 2 * c + 2)
                dve.wait_ge(s_pv, NU + g * NU + CHUNK_UNIT[c] + 1)
                v.tensor_tensor(OT[:, p, c * QC:c * QC + QW[c]],
                                O[:, c, 0:QW[c]], RC[:, c, 0:QW[c]], ALU.mult).then_inc(s_norm, 1)

            ROUTE_PARTS = 10

            def choose(b, part, done):
                if part == 0:
                    dve.wait_ge(s_evac, 1 + done + 1)
                    apart(dve)
                    several([v.max(top[:, t], lg[:, t]) for t in range(KT)])
                elif part == 1:
                    apart(dve)
                    several([v.max_index(ti[:, t], top[:, t], lg[:, t]) for t in range(KT)])
                elif part == 2:
                    v.tensor_tensor(eg[:, 1], top[:, :, 1], top[:, :, 0], ALU.subtract).then_inc(s_ge, 1)
                    link(v.tensor_copy(tf[:], ti[:, :, 0:2]))
                    several([v.tensor_tensor(M[:, k], iota_e[:], tf[:, :, k:k + 1].to_broadcast([P, KT, NE]),
                                             ALU.is_equal) for k in range(2)])
                elif part == 3:
                    several([v.tensor_tensor(M[:, k], M[:, k], valid[:], ALU.mult) for k in range(2)])
                    v.tensor_tensor(CC[:], M[:, 0], M[:, 1], ALU.add).then_inc(s_cc, 1)
                elif part == 4:
                    dve.wait_ge(s_ge, 2 * b + 2)
                    link(v.tensor_scalar(eg[:, 1], eg[:, 0], 1.0, None, ALU.add))
                    link(v.reciprocal(gate[:], eg[:, 1]))
                    link(v.tensor_tensor(XN[:, :, G2], gate[:], eg[:, 0], ALU.mult))
                elif part == 5:
                    several([v.tensor_tensor(XN[:, :, DG], gate[:], XN[:, :, G2], ALU.subtract),
                             v.tensor_copy(XN[:, :, E1], tf[:, :, 0]),
                             v.tensor_copy(XN[:, :, TOK], tok[:])])
                    link(v.tensor_scalar(tok[:], tok[:], float(T), None, ALU.add))
                elif part < 9:
                    if part == 6:
                        dve.wait_ge(s_evac, 1 + done + 1)
                        dve.wait_ge(s_dve, base[0] + count[0])
                    for t in range(3 * (part - 6), 3 * (part - 6) + 3):
                        several([v.tensor_tensor(rank[:, t], rk[:, NE * t:NE * t + NE], run[:], ALU.add)])
                        several([v.tensor_tensor(run[:], run[:], rk[:, 128 + NE * t:128 + NE * t + NE], ALU.add)])
                else:
                    link(v.scalar_tensor_tensor(out=rank[:], in0=iota_e[:], scalar=float(REGION),
                                                in1=rank[:], op0=ALU.mult, op1=ALU.add))
                    several([v.tensor_tensor(mr[:, k], M[:, k], rank[:], ALU.mult) for k in range(2)])
                    link(v.tensor_reduce(pf[:], mr[:], AX.X, ALU.add))
                    link(v.tensor_tensor(pf[:], pf[:], trash[:], ALU.add))
                    link(v.tensor_copy(pi[:], pf[:]))
                    dve.sem_inc(s_pos, 1)

            def wide(ap):
                return ap.rearrange("p (o e) -> p o e", o=1).to_broadcast([P, NTILE, NE])

            def list_tiles():
                dve.wait_ge(s_const, 15)
                link(v.tensor_tensor(cmp, run[:].rearrange("p (e o) -> p e o", o=1).to_broadcast([P, NE, MAXT]),
                                     thr, ALU.is_gt))
                link(v.tensor_reduce(ntiles, cmp, AX.X, ALU.add))
                link(v.tensor_copy(ci, ntiles))
                for e in range(1, NE):
                    link(v.tensor_tensor(ci[:, e:e + 1], ci[:, e:e + 1], ci[:, e - 1:e], ALU.add))
                link(v.tensor_tensor(ce, ci, ntiles, ALU.subtract))
                link(v.tensor_tensor(a, tid, wide(ci), ALU.is_ge))
                link(v.tensor_reduce(EF[:], a, AX.X, ALU.add))
                link(v.tensor_scalar(EF[:], EF[:], float(NE - 1), None, ALU.min))
                link(v.tensor_tensor(z, tid, wide(ce), ALU.is_ge))
                link(v.tensor_tensor(a, z, a, ALU.subtract))
                link(v.tensor_tensor(z, tid, wide(ce), ALU.subtract))
                link(v.scalar_tensor_tensor(out=z, in0=z, scalar=float(TT), in1=eid,
                                            op0=ALU.mult, op1=ALU.add))
                link(v.tensor_scalar(z, z, float(SPARE), None, ALU.subtract))
                link(v.tensor_tensor(z, z, a, ALU.mult))
                link(v.tensor_reduce(SF, z, AX.X, ALU.add))
                link(v.tensor_scalar(SF, SF, float(SPARE), None, ALU.add))
                link(v.tensor_copy(SI[:], SF))
                link(v.tensor_copy(EI[:], EF[:]))
                link(v.tensor_tensor(zf, run[:], eid[:, 0], ALU.add))
                link(v.tensor_copy(ZI[:], zf))
                dve.sem_inc(s_listed, 1)

            def take(i, q, kind, what, c):
                g, at = i * PAIRS + q, jobs_before(i, q) + index_of(kind, (what, c))
                if what == "den":
                    take_den(g - (c > 0), c, at)
                else:
                    read_out(what, c, 1 - q % 2, g + 1, at, i)

            def pair(i, q, kind, p):
                g, j = i * PAIRS + q, q % 2
                done = jobs_before(i, q)
                if q == LEAD:
                    base[0], count[0] = LEAD_CHAIN + i * CHAIN, 0
                for n in range(NS):
                    m = n - SUM_LAG
                    if 0 <= m < DSUMS:
                        den = DEN1 if m < 2 else DEN2
                        sums(g, j, m, done if kind == "first" else done + index_of(kind, den) + 1)
                    for what, c in JOBS[kind][n]:
                        take(i, q, kind, what, c)
                    if n in RECIP_AT and not (kind == "first" and n < 12):
                        c, half = RECIP_AT[n]
                        ago = int(c > 0)
                        normalise(g - ago, (p - ago) % PAIRS, c, half, done + index_of(kind, ("den", c)))
                    if kind == "norm" and 3 <= n < 3 + NORM_PARTS:
                        first_norm(i + 1, n - 3)
                    if kind == "out":
                        for what, c in JOBS[kind][n]:
                            if what == "o":
                                second_norm_stats(c, done + index_of(kind, (what, c)))
                    if kind == "norm2" and 3 <= n < NORM_PARTS:
                        second_norm(n)
                    if kind == "route":
                        if 4 <= n < 10:
                            choose(i, n - 4, done + index_of(kind, ("r", 0)))
                        elif n >= 10:
                            choose(i, n - 4, done + index_of(kind, ("n", 0)))
                assert q != LEAD + PAIRS - 1 or count[0] == CHAIN, count[0]

            def tail():
                g, at = B * PAIRS - 1, last_jobs
                for c in (1, 2):
                    take_den(g, c, at)
                    for half in range(2):
                        normalise(g, PAIRS - 1, c, half, at)
                    at += 1
                base[0], count[0] = LEAD_CHAIN + (B - 1) * CHAIN, 0
                for k, (what, c) in enumerate(NO_PAIR):
                    if what == "y" and c == 0:
                        for part in range(3, NORM_PARTS):
                            second_norm(part)
                    read_out(what, c, None, None, at, B - 1, bank=k)
                    if what == "o":
                        second_norm_stats(c, at)
                    if what in "rn":
                        for part in range(0, 6) if what == "r" else range(6, ROUTE_PARTS):
                            choose(B - 1, part, at)
                    at += 1
                list_tiles()

            for part in range(NORM_PARTS):
                first_norm(0, part)
            for k in range(TURN):
                read_out("x", k, None, None, k, None, bank=k)
            for k, (what, c) in enumerate(PROJ):
                read_out(what, c, 0, 0, TURN + k, None, bank=TURN + k)
            LEAD_CHAIN = count[0]
            rounds(dve, pair, tail)


def rsqrt_guess(v, link, var, y, h, t, eps):
    link(v.tensor_scalar(h[:], var, eps, None, ALU.add))
    link(v.tensor_scalar(t[:].bitcast(I32), h[:].bitcast(I32), 1, None, ALU.arith_shift_right))
    link(v.tensor_scalar(y[:].bitcast(I32), t[:].bitcast(I32), -1.0, float(0x5F3759DF), ALU.mult, ALU.add))
    link(v.tensor_scalar(h[:], h[:], -0.5, None, ALU.mult))


def rsqrt_newton(v, link, y, h, t, steps):
    for _ in range(steps):
        link(v.tensor_tensor(t[:], y[:], y[:], ALU.mult))
        link(v.tensor_tensor(t[:], t[:], h[:], ALU.mult))
        link(v.scalar_tensor_tensor(out=y[:], in0=t[:], scalar=1.5, in1=y[:], op0=ALU.add, op1=ALU.mult))


def experts(nc, io, xs, out, keep):
    w1, b1, w2, bc = io["w1"], io["b1"], io["w2"], io["bc"]
    ident, EF, EI, SI = (keep[k] for k in ("ident", "EF", "EI", "SI"))
    with ExitStack() as ctx:
        def sb(name, shape, dt=F32):
            return ctx.enter_context(nc.sbuf_tensor(name, shape, dt))

        def sem(name):
            return ctx.enter_context(nc.semaphore(name))

        def pair_of(name, shape, dt=F32):
            return [sb(f"{name}{j}", shape, dt) for j in range(2)]

        def sems(name):
            return [sem(f"{name}{j}") for j in range(2)]

        fill = sb("fill", [P, TS, D])
        XR = pair_of("XR", [P, TS, ROW])
        W1s = sb("W1s", [P, C * F])
        W2s = sb("W2s", [P, FM * D])
        W1 = pair_of("W1_", [P, 2, C * F], F32R)
        W2 = pair_of("W2_", [P, 2, FM * D], F32R)
        B1 = pair_of("B1_", [P, FM])
        BC = pair_of("BC_", [P, 3, D])
        xT = pair_of("xT_", [P, 2, C, TT], F32R)
        h32 = sb("h32", [P, HRING, TT])
        hT = sb("hT", [P, 2, FM, TT], F32R)
        XB = sb("XB", [P, TS, D])
        RES = sb("RES", [P, TS, D])
        NRM = sb("NRM", [P, TS, D])
        GM = sb("GM", [P, TS, D])
        OUT = pair_of("OUT_", [P, TS, D])
        IDX = pair_of("IDX_", [P, TS], I32)
        st = sb("st2", [P, TS, 6])
        mv = sb("mv2", [P, TS, 2])
        rs = sb("rs2", [P, TS])
        vh = sb("vh2", [P, TS])
        tt_ = sb("tt2", [P, TS])
        g = sb("g2", [P, TS])
        rg = sb("rg2", [P, TS])

        H1 = ctx.enter_context(nc.psum_tensor("H1", [P, 4, 512], F32))
        Y2 = ctx.enter_context(nc.psum_tensor("Y2", [P, TS, 512], F32))
        XP = ctx.enter_context(nc.psum_tensor("XP", [P, 512], F32))

        s_const = sem("e_const")
        s_x = sems("e_x")
        s_bc = sems("e_bc")
        s_w1s = sem("e_w1s")
        s_w2s = sem("e_w2s")
        s_wh = sem("e_wh")
        s_w1 = sem("e_w1")
        s_w2 = sem("e_w2")
        s_xp = sem("e_xp")
        s_xh = sem("e_xh")
        s_xT = sem("e_xT")
        s_m1 = sem("e_m1")
        s_ge = sem("e_ge")
        s_hl = sem("e_hl")
        s_m2 = sem("e_m2")
        s_xb = sem("e_xb")
        s_res = sem("e_res")
        s_ch = sem("e_ch")
        s_nrm = sem("e_nrm")
        s_gm = sem("e_gm")
        s_out = sem("e_out")
        s_apart = sem("e_apart")
        s_add = sem("e_add")
        s_clear = sem("e_clear")

        def apart(eng):
            eng.sem_inc(s_apart, 1)

        block = ctx.enter_context(nc.Block())
        HALF = NTILE // 2
        assert NTILE % 2 == 1
        WC = C * F // 4
        assert C * F == FM * D

        @block.sync
        def _(sp):
            def first_weights(t, first=False):
                if not first:
                    sp.wait_ge(s_w1, 8 * t)
                    apart(sp)
                e = sp.value_load(EI[0:1, bass.ds(t, 1)], min_val=0, max_val=NE - 1)
                sp.dma_start(W1s[:].rearrange("p (c f) -> p c f", c=C),
                             w1[bass.ds(e, 1)].rearrange("a (c p) f -> p (a c) f", p=P)).then_inc(s_w1s, 16)

            def second_weights(t, first=False):
                if not first:
                    sp.wait_ge(s_w2, 4 * t)
                    apart(sp)
                e = sp.value_load(EI[0:1, bass.ds(t, 1)], min_val=0, max_val=NE - 1)
                sp.dma_start(W2s[:].rearrange("p (m d) -> p m d", m=FM),
                             w2[bass.ds(e, 1)].rearrange("a (m p) d -> p (a m) d", p=P)).then_inc(s_w2s, 16)

            def rows(t, j, first=False):
                if not first:
                    sp.wait_ge(s_res, t)
                    apart(sp)
                row = sp.value_load(SI[0:1, bass.ds(t, 1)], min_val=0, max_val=SPARE)
                e = sp.value_load(EI[0:1, bass.ds(t, 1)], min_val=0, max_val=NE - 1)
                sp.dma_start(XR[j][:], xs[bass.ds(row, TT)].rearrange("(t p) d -> p t d", p=P)).then_inc(s_x[j], 16)
                sp.dma_start(B1[j][:], b1[bass.ds(e, 1)].rearrange("a p m -> p (a m)")).then_inc(s_x[j], 16)

            def vectors(t, j, first=False):
                if not first:
                    sp.wait_ge(s_out, t)
                    apart(sp)
                e = sp.value_load(EI[0:1, bass.ds(t, 1)], min_val=0, max_val=NE - 1)
                sp.dma_start(BC[j][:], bc[bass.ds(e, 1)].to_broadcast([P, 3, D])).then_inc(s_bc[j], 16)

            first_weights(0, first=True)
            rows(0, 0, first=True)
            second_weights(0, first=True)
            vectors(0, 0, first=True)
            rows(1, 1, first=True)
            vectors(1, 1, first=True)
            first_weights(1)
            second_weights(1)
            with sp.Fori(1, HALF) as k:
                for j in range(2):
                    first_weights(2 * k + j)
                    rows(2 * k + j, j)
                    second_weights(2 * k + j)
                    vectors(2 * k + j, j)
            first_weights(NTILE - 1)
            rows(NTILE - 1, 0)
            second_weights(NTILE - 1)
            vectors(NTILE - 1, 0)

        @block.gpsimd
        def _(pool):
            nc.gpsimd.memset(fill[:], 0.0).then_inc(s_const, 1)
            pool.wait_ge(s_const, 1)
            nc.gpsimd.dma_start(out[B * T:B * T + TT].rearrange("(t p) d -> p t d", p=P),
                                fill[:]).then_inc(s_add, 16)
            pool.sem_inc(s_gm, 1)
            pool.sem_inc(s_clear, 1)

            def bias(t, j, k):
                pool.wait_ge(s_x[j], 32 * (k + 1))
                pool.wait_ge(s_bc[j], 16 * (k + 1))
                pool.wait_ge(s_res, 1 + t)
                nc.gpsimd.tensor_tensor(XB[:], XR[j][:, :, 0:D], BC[j][:, 0:1].to_broadcast([P, TS, D]),
                                        ALU.add).then_inc(s_xb, 1)

            def low(t, j):
                for q in range(4):
                    cols = slice(q * WC, (q + 1) * WC)
                    pool.wait_ge(s_wh, 8 * t + 4 + q + 1)
                    nc.gpsimd.tensor_tensor(W2[j][:, 1, cols], W2s[:, cols], W2[j][:, 0, cols].bitcast(F32),
                                            ALU.subtract).then_inc(s_w2, 1)

            def scale(t, j):
                pool.wait_ge(s_nrm, t + 1)
                pool.wait_ge(s_out, t + 1)
                nc.gpsimd.tensor_tensor(GM[:], NRM[:], BC[j][:, 1:2].to_broadcast([P, TS, D]),
                                        ALU.mult).then_inc(s_gm, 1)

            def add(t, j):
                pool.wait_ge(s_out, 1 + t + 1)
                pool.wait_ge(s_add, 16 + 16 * TS * t)
                pool.sem_inc(s_clear, 1)
                for k in range(TS):
                    nc.gpsimd.indirect_dma_start(out, bass.IndirectOffsetOnAxis(IDX[j][:, k:k + 1], 0),
                                                 OUT[j][:, k], None, compute_op=ALU.add).then_inc(s_add, 16)

            def tile(t, j, k, last=False):
                bias(t, j, k)
                if not last:
                    low(t + 1, 1 - j)
                scale(t, j)
                add(t, j)

            low(0, 0)
            with pool.Fori(0, HALF) as k:
                tile(2 * k, 0, k)
                tile(2 * k + 1, 1, k)
            tile(NTILE - 1, 0, HALF, last=True)
            pool.wait_ge(s_add, 16 + 16 * TS * NTILE)

        @block.scalar
        def _(act):
            act.sem_inc(s_ge, 4)

            def high(t, j, w, q):
                src, dst, loaded = ((W1s, W1, s_w1s), (W2s, W2, s_w2s))[w]
                cols = slice(q * WC, (q + 1) * WC)
                if q == 0:
                    act.wait_ge(loaded, 16 * (t + 1))
                nc.scalar.copy(dst[j][:, 0, cols], src[:, cols]).then_inc(s_wh, 1)

            def x_high(t, j, c):
                act.wait_ge(s_xp, C * t + c + 1)
                nc.scalar.copy(xT[j][:, 0, c], XP[:, 0:TT]).then_inc(s_xh, 1)

            def prepare(t, j):
                x_high(t, j, 0)
                for q in range(4):
                    high(t, j, 0, q)
                x_high(t, j, 1)
                for q in range(4):
                    high(t, j, 1, q)

            def tile(t, j, k, last=False):
                act.wait_ge(s_x[j], 32 * (k + 1))
                for m in range(FM):
                    act.wait_ge(s_m1, FM * t + m + 1)
                    nc.scalar.activation(hT[:, 0, m], H1[:, m % 4, 0:TT], ACT.Gelu,
                                         bias=B1[j][:, m:m + 1]).then_inc(s_apart, 1)
                    act.wait_ge(s_hl, FM * t + m + 1)
                    nc.scalar.activation(h32[:, m % HRING], H1[:, m % 4, 0:TT], ACT.Gelu,
                                         bias=B1[j][:, m:m + 1]).then_inc(s_ge, 1)
                if not last:
                    prepare(t + 1, 1 - j)

            prepare(0, 0)
            with act.Fori(0, HALF) as k:
                tile(2 * k, 0, k)
                tile(2 * k + 1, 1, k)
            tile(NTILE - 1, 0, HALF, last=True)

        @block.tensor
        def _(pe):
            def turn(t, j, k, c):
                if c == 0:
                    pe.wait_ge(s_x[j], 32 * (k + 1))
                pe.wait_ge(s_xT, 1 + C * t + c)
                for i in range(TS):
                    mm = nc.tensor.transpose(XP[:, P * i:P * i + P], XR[j][:, i, P * c:P * c + P], ident[:])
                mm.then_inc(s_xp, 1)

            def tile(t, j, k, kn):
                pe.wait_ge(s_w1, 8 * (t + 1))
                pe.wait_ge(s_xT, 1 + C * t + C)
                for m in range(FM):
                    pe.wait_ge(s_ge, FM * t + m + 1)
                    for c in range(C):
                        w = [W1[j][:, part, c * F + P * m:c * F + P * m + P] for part in range(2)]
                        for n, (a_, b_) in enumerate(((0, 0), (0, 1), (1, 0))):
                            mm = nc.tensor.matmul(H1[:, m % 4, 0:TT], w[a_], xT[j][:, b_, c],
                                                  start=(c == 0 and n == 0), stop=(c == C - 1 and n == 2))
                    mm.then_inc(s_m1, 1)
                if kn is not None:
                    turn(t + 1, 1 - j, kn, 0)
                pe.wait_ge(s_res, 1 + t)
                pe.wait_ge(s_w2, 4 * (t + 1))
                for m in range(FM):
                    pe.wait_ge(s_hl, HRING + FM * t + m + 1)
                    for i in range(TS):
                        h = [hT[:, part, m, P * i:P * i + P] for part in range(2)]
                        for n, (a_, b_) in enumerate(((0, 0), (0, 1), (1, 0))):
                            mm = nc.tensor.matmul(Y2[:, i, 0:D], h[a_], W2[j][:, b_, D * m:D * m + D],
                                                  start=(m == 0 and n == 0), stop=(m == FM - 1 and n == 2))
                    if m == 5 and kn is not None:
                        turn(t + 1, 1 - j, kn, 1)
                mm.then_inc(s_m2, 1)

            turn(0, 0, 0, 0)
            turn(0, 0, 0, 1)
            with pe.Fori(0, HALF) as k:
                tile(2 * k, 0, k, k)
                tile(2 * k + 1, 1, k, k + 1)
            tile(NTILE - 1, 0, HALF, None)

        @block.vector
        def _(dve):
            v = nc.vector
            count = [0]
            base = [0]

            def link(ins):
                count[0] += 1
                ins.then_inc(s_ch, 1)
                dve.wait_ge(s_ch, base[0] + count[0])

            dve.sem_inc(s_xT, 1)
            dve.sem_inc(s_hl, HRING)
            dve.sem_inc(s_res, 1)
            dve.sem_inc(s_out, 1)

            def turned(t, j, c):
                dve.wait_ge(s_xh, C * t + c + 1)
                v.tensor_tensor(xT[j][:, 1, c], XP[:, 0:TT], xT[j][:, 0, c].bitcast(F32),
                                ALU.subtract).then_inc(s_xT, 1)

            def low(t, j, q):
                cols = slice(q * WC // 2, (q + 1) * WC // 2)
                dve.wait_ge(s_wh, 8 * t + q // 2 + 1)
                v.tensor_tensor(W1[j][:, 1, cols], W1s[:, cols], W1[j][:, 0, cols].bitcast(F32),
                                ALU.subtract).then_inc(s_w1, 1)

            def hidden_low(t, m):
                dve.wait_ge(s_ge, 4 + FM * t + m + 1)
                v.tensor_tensor(hT[:, 1, m], h32[:, m % HRING], hT[:, 0, m].bitcast(F32),
                                ALU.subtract).then_inc(s_hl, 1)

            def several(ops):
                for ins in ops[:-1]:
                    ins.then_inc(s_ch, 1)
                    count[0] += 1
                link(ops[-1])

            FINISH = 5

            def finish(t, j, part):
                if part == 0:
                    base[0], count[0] = t * ECHAIN, 0
                    dve.wait_ge(s_out, 1 + t)
                    link(v.tensor_scalar(g[:], XR[j][:, :, E1], EF[:, bass.ds(t, 1)], None, ALU.is_equal))
                    link(v.tensor_tensor(g[:], g[:], XR[j][:, :, DG], ALU.mult))
                    link(v.tensor_tensor(g[:], g[:], XR[j][:, :, G2], ALU.add))
                    dve.wait_ge(s_clear, 1 + t)
                    link(v.tensor_copy(IDX[j][:], XR[j][:, :, TOK]))
                    dve.wait_ge(s_xb, t + 1)
                    dve.wait_ge(s_m2, t + 1)
                    v.tensor_tensor(RES[:], Y2[:, :, 0:D], XB[:], ALU.add).then_inc(s_res, 1)
                    dve.wait_ge(s_res, 1 + t + 1)
                    several([v.bn_stats(st[:, i], RES[:, i]) for i in range(TS)])
                elif part == 1:
                    apart(dve)
                    several([v.bn_aggr(mv[:, i], st[:, i]) for i in range(TS)])
                    rsqrt_guess(v, link, mv[:, :, 1], rs, vh, tt_, LN2_EPS)
                    rsqrt_newton(v, link, rs, vh, tt_, 1)
                elif part == 2:
                    rsqrt_newton(v, link, rs, vh, tt_, 2)
                    link(v.tensor_tensor(rg[:], rs[:], g[:], ALU.mult))
                elif part == 3:
                    dve.wait_ge(s_gm, 1 + t)
                    ops = [v.tensor_scalar(NRM[:, i], RES[:, i], mv[:, i, 0:1], rg[:, i:i + 1],
                                           ALU.subtract, ALU.mult) for i in range(TS)]
                    ops[-1].then_inc(s_nrm, 1)
                    for ins in ops[:-1]:
                        ins.then_inc(s_ch, 1)
                else:
                    dve.wait_ge(s_gm, 1 + t + 1)
                    ops = [v.scalar_tensor_tensor(out=OUT[j][:, i], in0=BC[j][:, 2], scalar=g[:, i:i + 1],
                                                  in1=GM[:, i], op0=ALU.mult, op1=ALU.add) for i in range(TS)]
                    ops[-1].then_inc(s_out, 1)
                    for ins in ops[:-1]:
                        ins.then_inc(s_ch, 1)
                    count[0] += 2 * (TS - 1)
                    assert count[0] == ECHAIN, count[0]

            FINISH_AT = {0: (0, 1), 1: (2,), 2: (3,), 5: (4,)}

            def tile(t, j, last=False, first=False):
                for m in range(FM):
                    if not first:
                        for part in FINISH_AT.get(m, ()):
                            finish(t - 1, 1 - j, part)
                    hidden_low(t, m)
                if not last:
                    turned(t + 1, 1 - j, 0)
                    for q in range(8):
                        low(t + 1, 1 - j, q)
                    turned(t + 1, 1 - j, 1)

            turned(0, 0, 0)
            for q in range(8):
                low(0, 0, q)
            turned(0, 0, 1)
            tile(0, 0, first=True)
            with dve.Fori(0, HALF - 1) as k:
                tile(2 * k + 1, 1)
                tile(2 * k + 2, 0)
            tile(NTILE - 2, 1)
            tile(NTILE - 1, 0, last=True)
            for part in range(FINISH):
                finish(NTILE - 1, 0, part)


def build(nc, io, xs, out):
    with ExitStack() as ctx:
        def sb(name, shape, dt=F32):
            return ctx.enter_context(nc.sbuf_tensor(name, shape, dt))

        keep = {
            "run": sb("run", [P, NE]),
            "ident": sb("ident", [P, P]),
            "EF": sb("EF", [P, NTILE]),
            "EI": sb("EI", [P, NTILE], I32),
            "SI": sb("SI", [P, NTILE], I32),
        }
        attention(nc, io, xs, out, keep)
        experts(nc, io, xs, out, keep)


def kernel(x, cls_tok, L0_tok_W1, L0_tok_b1, L0_tok_W2, L0_tok_b2, L0_attn_Wq, L0_attn_Wk, L0_attn_Wv,
           L0_attn_Wo, L0_ffn_router_w, L0_ffn_w1, L0_ffn_b1, L0_ffn_w2, L0_ffn_b2, L0_ffn_gamma,
           L0_ffn_beta):
    import numpy as np
    import concourse.bacc as bacc
    from concourse.bass_utils import run_bass_kernel_spmd

    def by_pair(w):
        return np.asarray(w).reshape(PAIRS, P, C, P).transpose(0, 3, 2, 1)

    wqkv = np.stack([by_pair(w) for w in (L0_attn_Wq, L0_attn_Wk, L0_attn_Wv)], axis=2)
    arrays = {
        "x": np.asarray(x).reshape(B, X, D),
        "cls": np.asarray(cls_tok).reshape(1, D),
        "wqkv": wqkv,
        "wot": np.asarray(L0_attn_Wo).T.reshape(PAIRS, P, D).transpose(1, 0, 2),
        "router": np.asarray(L0_ffn_router_w).reshape(C, P, NE).transpose(1, 0, 2),
        "w1": np.asarray(L0_ffn_w1),
        "b1": np.asarray(L0_ffn_b1).reshape(NE, FM, P).transpose(0, 2, 1),
        "w2": np.asarray(L0_ffn_w2),
        "bc": np.stack([np.asarray(a) for a in (L0_ffn_b2, L0_ffn_gamma, L0_ffn_beta)], axis=1),
    }
    arrays = {k: np.ascontiguousarray(a) for k, a in arrays.items()}
    nc = bacc.Bacc("TRN2", target_bir_lowering=False, num_devices=1)
    io = {k: nc.dram_tensor(f"in_{k}", list(a.shape), F32, kind="ExternalInput").ap() for k, a in arrays.items()}
    xs = nc.dram_tensor("rows", [ROWS, ROW], F32, kind="Internal").ap()
    out = nc.dram_tensor("out", [B * T + TT, D], F32, kind="ExternalOutput").ap()
    build(nc, io, xs, out)
    r = run_bass_kernel_spmd(nc, [{f"in_{k}": a for k, a in arrays.items()}], core_ids=[0])
    return r.results[0]["out"][0:B * T].reshape(B, T, D)
```
